# Optimizing a Trainium2 kernel written in Bass

```python
import numpy as np
import jax
import jax.numpy as jnp

def _softmax(x, axis=-1):
    return jax.nn.softmax(x, axis=axis)

def _gelu(x):
    return jax.nn.gelu(x, approximate=True)

def _silu(x):
    return jax.nn.silu(x)

def _sigmoid(x):
    return jax.nn.sigmoid(x)

def _layernorm(x, axis=-1, eps=1e-05):
    m = jnp.mean(x, axis=axis, keepdims=True)
    v = jnp.var(x, axis=axis, keepdims=True)
    return (x - m) / jnp.sqrt(v + eps)

def _scatter_add(tgt, idx, src, axis=0):
    return tgt.at[idx].add(src)

def _segment_sum(src, seg, n):
    return jax.ops.segment_sum(src, seg, n)
kernel_name = 'mk_flamingo_gated_d1_seqx_r2_026acd'

def setup_inputs(seed: int=0):
    np.random.seed(seed)
    _w = jnp.asarray

    def _rec_inputs():
        import jax
        import jax.numpy as jnp
        _rk = jax.random.key(seed)
        x = -0.000125 + 0.9999 * jax.random.normal(jax.random.fold_in(_rk, 1), (2, 1024, 2048), jnp.float32)
        _lenS = 1024 - jax.random.randint(jax.random.fold_in(_rk, 7), (2,), 0, max(1, 1024 // 4) + 1, jnp.int32)
        _lenS2 = 2048 - jax.random.randint(jax.random.fold_in(_rk, 8), (2,), 0, max(1, 2048 // 4) + 1, jnp.int32)
        _ctx_4096P = jax.random.normal(jax.random.fold_in(_rk, 11), (2, 16, 2048), jnp.float32)
        _ctx_4096c = jax.random.dirichlet(jax.random.fold_in(_rk, 511), 0.3 * jnp.ones((16,), jnp.float32), (2, 2048))
        _ctx_4096t = jnp.einsum('bsk,bkd->bsd', _ctx_4096c, _ctx_4096P)
        _ctx_4096t = _ctx_4096t * jax.lax.rsqrt(jnp.mean(jnp.square(_ctx_4096t)) + 1e-12) * 0.953939
        ctx_4096 = -5.72187e-05 + 0.999849 * (_ctx_4096t + 0.3 * jax.random.normal(jax.random.fold_in(_rk, 611), (2, 2048, 2048), jnp.float32))
        _g = jax.random.normal(jax.random.fold_in(_rk, 9001), (2, 1), jnp.float32)
        _g = jnp.sign(_g) * jnp.maximum(jnp.abs(_g), 1.0) + (_g == 0) * 1.0
        g_xattn = _g[0]
        g_ffn = _g[1]
        return (x, ctx_4096, g_xattn, g_ffn)
    x, ctx_4096, g_xattn, g_ffn = _rec_inputs()

    def _L0_xattn_setup():
        import jax, jax.numpy as jnp
        import numpy as np
        QMIN = 0.0
        QMAX = 255.0

        def fake_quant(x, scale, zp):
            s = scale.reshape(())
            z = zp.reshape(())
            q = jnp.clip(jnp.round(x / s + z), QMIN, QMAX)
            return (q - z) * s
        key = jax.random.key(seed)
        k1, k2 = jax.random.split(key)
        B, M, K, N = (4, 1024, 2048, 2048)
        x1 = jax.random.normal(k1, (B, M, K), dtype=jnp.float32)
        x2 = jax.random.normal(k2, (B, K, N), dtype=jnp.float32)
        x1_scale = jnp.full((1,), 8.0 / 255.0, dtype=jnp.float32)
        x1_zp = jnp.full((1,), 128.0, dtype=jnp.float32)
        x2_scale = jnp.full((1,), 8.0 / 255.0, dtype=jnp.float32)
        x2_zp = jnp.full((1,), 128.0, dtype=jnp.float32)
        return {'x1': x1, 'x2': x2, 'x1_scale': x1_scale, 'x1_zp': x1_zp, 'x2_scale': x2_scale, 'x2_zp': x2_zp}
    _L0_xattn_all = _L0_xattn_setup()
    _L0_xattn_in = {k: v for k, v in _L0_xattn_all.items() if k in ('x1_scale', 'x1_zp', 'x2_scale', 'x2_zp')}
    del _L0_xattn_all

    def _L0_ffn_setup():
        import jax, jax.numpy as jnp
        import numpy as np
        OUT, IN, RANK = (2048, 2048, 512)
        B, T = (4, 2048)
        key = jax.random.key(seed)
        kx, ku, ks, kv = jax.random.split(key, 4)
        x = jax.random.normal(kx, (B, T, IN), dtype=jnp.float32)
        U = jax.random.normal(ku, (OUT, RANK), dtype=jnp.float32) / np.sqrt(OUT)
        S = jax.random.uniform(ks, (RANK,), dtype=jnp.float32, minval=0.1, maxval=10.0)
        S = jnp.sort(S)[::-1]
        V = jax.random.normal(kv, (IN, RANK), dtype=jnp.float32) / np.sqrt(IN)
        return {'x': x, 'U': U, 'S': S, 'V': V}
    _L0_ffn_all = _L0_ffn_setup()
    _L0_ffn_in = {k: v for k, v in _L0_ffn_all.items() if k in ('U', 'S', 'V')}
    del _L0_ffn_all
    return {'x': x, 'ctx_4096': ctx_4096, 'g_xattn': g_xattn, 'g_ffn': g_ffn, 'L0_xattn_x1_scale': _L0_xattn_in['x1_scale'], 'L0_xattn_x1_zp': _L0_xattn_in['x1_zp'], 'L0_xattn_x2_scale': _L0_xattn_in['x2_scale'], 'L0_xattn_x2_zp': _L0_xattn_in['x2_zp'], 'L0_ffn_U': _L0_ffn_in['U'], 'L0_ffn_S': _L0_ffn_in['S'], 'L0_ffn_V': _L0_ffn_in['V']}

def reference(x, ctx_4096, g_xattn, g_ffn, L0_xattn_x1_scale, L0_xattn_x1_zp, L0_xattn_x2_scale, L0_xattn_x2_zp, L0_ffn_U, L0_ffn_S, L0_ffn_V):
    import jax
    import jax.numpy as jnp

    def _L0_xattn_ref(x1, x2, x1_scale, x1_zp, x2_scale, x2_zp):
        import jax, jax.numpy as jnp
        import numpy as np
        QMIN = 0.0
        QMAX = 255.0

        def fake_quant(x, scale, zp):
            s = scale.reshape(())
            z = zp.reshape(())
            q = jnp.clip(jnp.round(x / s + z), QMIN, QMAX)
            return (q - z) * s
        q1 = fake_quant(x1, x1_scale, x1_zp)
        q2 = fake_quant(x2, x2_scale, x2_zp)
        return jnp.matmul(q1, q2)

    def _L0_ffn_ref(x, U, S, V):
        import jax, jax.numpy as jnp
        import numpy as np
        OUT, IN, RANK = (2048, 2048, 512)
        B, T = (4, 2048)
        weight = U * S[None, :] @ V.T
        return jnp.einsum('bti,oi->bto', x, weight)
    x = x + jnp.tanh(g_xattn[0]) * _L0_xattn_ref(_layernorm(x, axis=-1), ctx_4096, L0_xattn_x1_scale, L0_xattn_x1_zp, L0_xattn_x2_scale, L0_xattn_x2_zp)
    x = x + jnp.tanh(g_ffn[0]) * _L0_ffn_ref(_layernorm(x, axis=-1), L0_ffn_U, L0_ffn_S, L0_ffn_V)
    return x

_drawn_inputs = setup_inputs


def setup_inputs(seed=0):
    import zlib

    import numpy as np

    out = dict(_drawn_inputs(seed))
    spreads = {}
    factors = {}
    for name, (base, spread) in spreads.items():
        noise = np.random.default_rng([zlib.crc32(name.encode()), seed]).standard_normal(out[name].shape)
        drawn = base * np.exp(spread * noise) if base else spread * noise
        out[name] = jnp.asarray(drawn.astype(out[name].dtype))
    for name, factor in factors.items():
        out[name] = (out[name] * factor).astype(out[name].dtype)
    return out
```

```python
import concourse.bass as bass
from concourse import mybir
from contextlib import ExitStack


def gated_block_program(nc, x, ctx_in, g_xattn, g_ffn, s1, z1, s2, z2, U, S, V, out):
    f32, bf16, f16, i32 = mybir.dt.float32, mybir.dt.bfloat16, mybir.dt.float16, mybir.dt.int32
    ALU, ACT, AX = mybir.AluOpType, mybir.ActivationFunctionType, mybir.AxisListType

    P = 128
    NB, SEQ, D = x.shape
    RANK = V.shape[1]
    KT = D // P
    RT = RANK // P
    W = 512
    NQ = D // W
    TB = SEQ // P
    NT = NB * TB
    CK = 2
    CQ = KT // CK
    CB = NQ * CQ
    NST = 4
    EPS = 1e-5
    MAGIC = 1.5 * 2.0 ** 23
    XS = 2.0 ** 9
    WS = 2.0 ** 14
    HS = 2.0 ** -15

    x_rows = x.rearrange("b s d -> (b s) d")
    out_rows = out.rearrange("b s d -> (b s) d")
    ctx_k = ctx_in.rearrange("b (k p) n -> b p k n", p=P)
    V_k = V.rearrange("(k p) r -> p k r", p=P)
    U_o = U.rearrange("(o p) r -> p o r", p=P)

    es = ExitStack()
    with es:
        def sb(name, shape, dt):
            return es.enter_context(nc.sbuf_tensor(name, shape, dt))

        def sem(name):
            return es.enter_context(nc.semaphore(name))

        q2 = sb("q2", [P, NQ, KT, W], bf16)
        v_hl = sb("v_hl", [P, KT, 2, W], f16)
        u_hl = sb("u_hl", [P, NQ, RT, 2, W], f16)
        ring = sb("ring", [P, 3, D], f32)
        qT = sb("qT", [P, 2, KT, P], bf16)
        xT_hi = sb("xT_hi", [P, KT, P], f16)
        xT_lo = sb("xT_lo", [P, KT, P], f16)
        piece = sb("piece", [P, 3, W], f32)
        qn = sb("qn", [P, 2, W], bf16)
        stage = sb("stage", [P, NST, CK, W], f32)
        hT_hi = sb("hT_hi", [P, RT, P], f16)
        hT_lo = sb("hT_lo", [P, RT, P], f16)
        corr = sb("corr", [P, D], f32)
        ident_f = sb("ident_f", [P, P], f32)
        ident_b = sb("ident_b", [P, P], bf16)
        ones_f = sb("ones_f", [P, P], f32)
        ones_b = sb("ones_b", [P, P], bf16)
        par = sb("par", [P, 6], f32)
        s_col = sb("s_col", [P, RT], f32)
        const = sb("const", [P, 24], f32)
        st1 = sb("st1", [P, NQ, 6], f32)
        st2 = sb("st2", [P, 2, NQ, 6], f32)
        ln1 = sb("ln1", [P, 8], f32)
        ln2 = sb("ln2", [P, 2, 8], f32)
        r1p = sb("r1p", [P, 2, NQ], f32)
        bvec = sb("bvec", [P, 2, 2], f32)
        ssq = sb("ssq", [P, 2, 8], f32)
        wsc = sb("wsc", [P, 2, 4], f32)

        def bank(name):
            return es.enter_context(nc.psum_tensor(name, [P, W], f32))

        acc = [bank("acc0"), bank("acc1")]
        hP = bank("hP")
        yP = [bank("y0"), bank("y1")]
        T = [bank("t0"), bank("t1"), bank("t2")]

        v_raw = v_hl[:, :, :, :].rearrange("p k a w -> p k (a w)").bitcast(f32)
        u_raw = u_hl[:, :, :, :, :].rearrange("p n r a w -> p (n r) (a w)").bitcast(f32)
        split_tmp = [t[:, 8 * i:8 * i + 8, :].rearrange("p k w -> p (k w)")
                     for t in (xT_hi, xT_lo) for i in range(2)]
        junk = qn[:, :, :].rearrange("p a w -> p (a w)")

        (C_R1, C_R2, C_C1, C_C2, C_MC1, C_MC2, C_F1, C_F2, C_A, C_AF1, C_AF2, C_AFF, C_TG1, C_TG2,
         C_CY, C_T0, C_T1, C_Z1, C_EPS, C_ZERO) = [const[:, i:i + 1] for i in range(20)]
        P_S1, P_Z1, P_S2, P_Z2, P_G1, P_G2 = [par[:, i:i + 1] for i in range(6)]

        par_in = sem("par_in")
        x_in = sem("x_in")
        stage_in = [sem(f"stage_in{i}") for i in range(NST)]
        v_in = sem("v_in")
        y_stored = sem("y_stored")
        setup_ready = sem("setup_ready")
        tanh_ready = sem("tanh_ready")
        const_step = sem("const_step")
        ctx_scaled = sem("ctx_scaled")
        ctx_round = sem("ctx_round")
        q2_ready = sem("q2_ready")
        colsum_done = sem("colsum_done")
        corr_ready = sem("corr_ready")
        ln1_step = sem("ln1_step")
        ln1_sqrt = sem("ln1_sqrt")
        ln1_agg = sem("ln1_agg")
        ln1_agg2 = sem("ln1_agg2")
        st2_ready = sem("st2_ready")
        ln2_step = sem("ln2_step")
        ln2_sqrt = sem("ln2_sqrt")
        q_relu = sem("q_relu")
        q_round = sem("q_round")
        q_ready = sem("q_ready")
        t_written = sem("t_written")
        t_read = sem("t_read")
        row_step = sem("row_step")
        xc_ready = sem("xc_ready")
        s1_done = sem("s1_done")
        x1_ready = sem("x1_ready")
        xs_ready = sem("xs_ready")
        t_hi = sem("t_hi")
        mm3_done = sem("mm3_done")
        h_evac = sem("h_evac")
        y_done = sem("y_done")
        y_ready = sem("y_ready")
        sq_done = sem("sq_done")
        norm_sum = sem("norm_sum")
        norm_step = sem("norm_step")
        norm_sqrt = sem("norm_sqrt")
        split_hi = sem("split_hi")
        split_lo = sem("split_lo")
        split_copied = sem("split_copied")
        ut_done = sem("ut_done")
        ut_raw = sem("ut_raw")

        def base(u):
            return 2 * NQ + (2 * NQ + 1) * u - (NQ if u == NT - 1 else 0)

        def x_piece(u, p):
            return base(u) + p

        def h_piece(u):
            return base(u) + NQ

        def q_piece(t, j):
            return NQ * t + j if t < 2 else base(t - 2) + NQ + 1 + j

        def s1_unit(t, n):
            b, m = t // TB, t % TB
            return NQ * TB * b + (2 * n + m if m < 2 else NQ * m + n)

        def stage_count(c):
            extra = (D // P // CK) // NST if c >= CB else 0
            return 16 * (c // NST + 1 + extra)

        NU = D // P // CK
        N_CONST = 16
        has_s1 = lambda u: u % TB not in (0, TB - 1)
        xq = lambda t, n: ring[:, t % 3, n * W:(n + 1) * W]
        tiles_of = lambda b: (TB * b, TB * b + 1)

        block = es.enter_context(nc.Block())

        @block.gpsimd
        def _(pool):
            nc.gpsimd.memset(ident_f[:, :], 0.0)
            nc.gpsimd.memset(ident_b[:, :], 0.0)
            nc.gpsimd.memset(ones_f[:, :], 1.0)
            nc.gpsimd.memset(ones_b[:, :], 1.0).then_inc(setup_ready, 1)
            pool.wait_ge(setup_ready, 1)
            for m in (ident_f, ident_b):
                nc.gpsimd.affine_select(out=m[:, :], in_=m[:, :], compare_op=ALU.not_equal, fill=1.0,
                                        base=0, pattern=[[-1, P]], channel_multiplier=1)\
                    .then_inc(setup_ready, 1)
            for i in range(2 * KT):
                pool.wait_ge(split_lo, i + 1)
                dst = v_raw[:, i, :] if i < KT else u_raw[:, i - KT, :]
                nc.gpsimd.tensor_copy(dst, split_tmp[i % 4].bitcast(f32)).then_inc(split_copied, 1)

        @block.sync
        def _(sp):
            def load_x(t):
                if t >= 3:
                    sp.wait_ge(y_stored, 32 * (t - 2))
                if t >= 1:
                    sp.wait_ge(x_in, 16 * t)
                sp.dma_start(ring[:, t % 3, :], x_rows[t * P:(t + 1) * P, :]).then_inc(x_in, 16)

            def load_chunks(b, n):
                for i in range(CQ):
                    c = CB * b + CQ * n + i
                    if NST <= c < CB or c >= CB + NST:
                        sp.wait_ge(q2_ready, c - NST + 1)
                    elif c >= CB:
                        sp.wait_ge(ut_done, NQ * RT)
                    sp.dma_start(stage[:, c % NST, :, :],
                                 ctx_k[b, :, CK * i:CK * i + CK, n * W:(n + 1) * W])\
                        .then_inc(stage_in[c % NST], 16)

            load_x(0)
            for i, a in enumerate((s1, z1, s2, z2, g_xattn, g_ffn)):
                with nc.allow_non_contiguous_dma(reason="one scalar to all partitions"):
                    sp.dma_start(par[:, i:i + 1], a.rearrange("(o a) -> o a", o=1).to_broadcast([P, 1]))\
                        .then_inc(par_in, 16)
            with nc.allow_non_contiguous_dma(reason="512 scales"):
                sp.dma_start(s_col[:, :], S.rearrange("(r p) -> p r", p=P)).then_inc(par_in, 16)
            load_chunks(0, 0)
            load_x(1)
            for n in range(1, NQ):
                load_chunks(0, n)
            for i in range(4):
                sp.dma_start(v_raw[:, 4 * i:4 * i + 4, :], V_k[:, 4 * i:4 * i + 4, :]).then_inc(v_in, 16)
            load_x(2)
            for i in range(NU):
                if i < NST:
                    sp.wait_ge(q2_ready, CB - NST + i + 1)
                else:
                    sp.wait_ge(ut_done, RT * ((i - NST) // 2 + 1))
                sp.dma_start(stage[:, i % NST, :, :], U_o[:, CK * i:CK * i + CK, :])\
                    .then_inc(stage_in[i % NST], 16)
            for u in range(NT - 3):
                if u % TB == TB - 2:
                    load_chunks(u // TB + 1, 0)
                if u % TB == TB - 1:
                    for n in range(1, NQ):
                        load_chunks(u // TB + 1, n)
                load_x(u + 3)

        @block.tensor
        def _(pe):
            def q_transpose(t, j):
                i = q_piece(t, j)
                pe.wait_ge(q_ready, NQ * t + j + 1)
                if i >= 3:
                    pe.wait_ge(t_read, i - 2)
                dst = T[i % 3][:, 0:W // 2].bitcast(bf16)
                for k in range(4):
                    mm = nc.tensor.transpose(dst[:, k * P:(k + 1) * P], qn[:, j % 2, k * P:(k + 1) * P], ident_b[:, :])
                mm.then_inc(t_written, 1)

            def f_transpose(i):
                pe.wait_ge(t_read, i - 2)
                for k in range(4):
                    mm = nc.tensor.transpose(T[i % 3][:, k * P:(k + 1) * P], piece[:, i % 3, k * P:(k + 1) * P],
                                             ident_f[:, :])
                mm.then_inc(t_written, 1)

            def x_transpose(u, p):
                pe.wait_ge(xs_ready, NQ * u + p + 1)
                f_transpose(x_piece(u, p))

            def colsum(b, n):
                if b == 0 and n == 0:
                    pe.wait_ge(setup_ready, 3)
                if n == 0 and b > 0:
                    pe.wait_ge(h_evac, TB * b)
                if n > 0 or b > 0:
                    pe.wait_ge(corr_ready, NQ * b + n)
                for k in range(KT):
                    if k % CK == 0:
                        pe.wait_ge(q2_ready, CB * b + CQ * n + k // CK + 1)
                    mm = nc.tensor.matmul(hP[:, :], ones_b[:, :], q2[:, n, k, :], start=(k == 0), stop=(k == KT - 1))
                mm.then_inc(colsum_done, 1)

            def s1_part(t, n, k0, k1):
                i = s1_unit(t, n)
                if k0 == 0:
                    pe.wait_ge(t_read, q_piece(t, NQ - 1) + 1)
                    if i >= 2:
                        pe.wait_ge(x1_ready, i - 1)
                for k in range(k0, k1):
                    mm = nc.tensor.matmul(acc[i % 2][:, :], qT[:, t % 2, k, :], q2[:, n, k, :],
                                          start=(k == 0), stop=(k == KT - 1))
                if k1 == KT:
                    mm.then_inc(s1_done, 1)

            def mm3(u):
                pe.wait_ge(corr_ready, NQ * (u // TB + 1))
                if u >= 1:
                    pe.wait_ge(h_evac, u)
                for k in range(KT):
                    if k % 4 == 0:
                        pe.wait_ge(t_read, x_piece(u, k // 4) + 1)
                    nc.tensor.matmul(hP[:, :], xT_hi[:, k, :], v_hl[:, k, 0, :], start=(k == 0), stop=False)
                    nc.tensor.matmul(hP[:, :], xT_hi[:, k, :], v_hl[:, k, 1, :], start=False, stop=False)
                    mm = nc.tensor.matmul(hP[:, :], xT_lo[:, k, :], v_hl[:, k, 0, :], start=False, stop=(k == KT - 1))
                mm.then_inc(mm3_done, 1)

            def mm4(u, n):
                i = NQ * u + n
                if n == 0:
                    pe.wait_ge(t_read, h_piece(u) + 1)
                if i >= 2:
                    pe.wait_ge(y_ready, i - 1)
                for r in range(RT):
                    nc.tensor.matmul(yP[i % 2][:, :], hT_hi[:, r, :], u_hl[:, n, r, 0, :], start=(r == 0), stop=False)
                    nc.tensor.matmul(yP[i % 2][:, :], hT_hi[:, r, :], u_hl[:, n, r, 1, :], start=False, stop=False)
                    mm = nc.tensor.matmul(yP[i % 2][:, :], hT_lo[:, r, :], u_hl[:, n, r, 0, :],
                                          start=False, stop=(r == RT - 1))
                mm.then_inc(y_done, 1)

            def pair(b):
                t0, t1 = tiles_of(b)
                if b == 0:
                    pe.wait_ge(setup_ready, 3)
                    for j in range(NQ):
                        q_transpose(t0, j)
                for n in range(NQ):
                    colsum(b, n)
                    s1_part(t0, n, 0, KT)
                    if b == 0 and n == 0:
                        for j in range(NQ):
                            q_transpose(t1, j)
                    s1_part(t1, n, 0, KT)

            def weights():
                pe.wait_ge(sq_done, 8)
                pe.wait_ge(corr_ready, NQ)
                nc.tensor.matmul(hP[:, 0:8], ones_f[:, :], ssq[:, 0, :], start=True, stop=True).then_inc(norm_sum, 1)
                for n in range(NQ):
                    for i in (2 * n, 2 * n + 1):
                        pe.wait_ge(stage_in[i % NST], 16 * (CB // NST + i // NST + 1))
                    for r in range(RT):
                        q = RT * n + r
                        if q >= 2:
                            pe.wait_ge(ut_raw, q - 1)
                        for k in range(4):
                            i = 2 * n + k // 2
                            mm = nc.tensor.transpose(yP[q % 2][:, k * P:(k + 1) * P],
                                                     stage[:, i % NST, k % 2, r * P:(r + 1) * P], ident_f[:, :])
                        mm.then_inc(ut_done, 1)
                pe.wait_ge(sq_done, 16)
                pe.wait_ge(norm_step, 1)
                nc.tensor.matmul(hP[:, 0:8], ones_f[:, :], ssq[:, 1, :], start=True, stop=True).then_inc(norm_sum, 1)
                pe.wait_ge(split_copied, 2 * KT)
                pe.wait_ge(norm_step, 6)

            def stage2_block(u):
                t = u + 1
                if has_s1(u):
                    for n in range(NQ - 1):
                        s1_part(t, n, 0, KT)
                        x_transpose(u, n)
                    x_transpose(u, NQ - 1)
                else:
                    for p in range(NQ):
                        x_transpose(u, p)
                mm3(u)
                if has_s1(u):
                    s1_part(t, NQ - 1, 0, KT // 2)
                pe.wait_ge(h_evac, u + 1)
                f_transpose(h_piece(u))
                if has_s1(u):
                    s1_part(t, NQ - 1, KT // 2, KT)
                q = u + 2 < NT
                for n in range(NQ):
                    mm4(u, n)
                    if q and n < 2:
                        q_transpose(u + 2, n)
                    if q and n == 2:
                        q_transpose(u + 2, 2)
                        q_transpose(u + 2, 3)

            for b in range(NB):
                pair(b)
                if b == 0:
                    weights()
                for u in range(TB * b, TB * b + TB):
                    stage2_block(u)

        @block.scalar
        def _(act):
            def chunks(cs):
                for c in cs:
                    act.wait_ge(stage_in[c % NST], stage_count(c))
                    a = stage[:, c % NST, :, :]
                    nc.scalar.activation(a, a, ACT.Relu, bias=P_Z2, scale=C_R2).then_inc(ctx_scaled, 1)

            def sqrt1(t):
                act.wait_ge(ln1_step, 6 * t + 2)
                nc.scalar.activation(ln1[:, 3:4], ln1[:, 2:3], ACT.Sqrt).then_inc(ln1_sqrt, 1)

            def sqrt2(u):
                act.wait_ge(ln2_step, 6 * u + 2)
                nc.scalar.activation(ln2[:, u % 2, 3:4], ln2[:, u % 2, 2:3], ACT.Sqrt).then_inc(ln2_sqrt, 1)

            def relu(t, j):
                i = q_piece(t, j)
                act.wait_ge(ln1_step, 6 * t + 6)
                if i >= 3:
                    act.wait_ge(t_written, i - 2)
                nc.scalar.activation(piece[:, i % 3, :], xq(t, j), ACT.Relu, bias=ln1[:, 6:7], scale=ln1[:, 5:6])\
                    .then_inc(q_relu, 1)

            def centre(t, j):
                i = q_piece(t, j)
                act.wait_ge(q_round, NQ * t + j + 1)
                if NQ * t + j >= 2:
                    ip = q_piece(t, j - 2) if j >= 2 else q_piece(t - 1, j + 2)
                    act.wait_ge(t_written, ip + 1)
                if t >= 2:
                    act.wait_ge(row_step, 2 * (t - 1))
                nc.scalar.activation(qn[:, j % 2, :], piece[:, i % 3, :], ACT.Identity, bias=C_MC1,
                                     accum_out=r1p[:, t % 2, j:j + 1]).then_inc(q_ready, 1)

            def hi(i, dst):
                act.wait_ge(t_written, i + 1)
                nc.scalar.activation(dst, T[i % 3][:, :], ACT.Copy).then_inc(t_hi, 1)

            def h_out(u):
                i = h_piece(u)
                act.wait_ge(mm3_done, u + 1)
                act.wait_ge(t_written, i - 2)
                nc.scalar.activation(piece[:, i % 3, :], hP[:, :], ACT.Copy, scale=HS).then_inc(h_evac, 1)

            def squares(w):
                src = (v_raw if w == 0 else u_raw)
                for i in range(8):
                    if 8 * w + i:
                        act.wait_ge(sq_done, 8 * w + i)
                    nc.scalar.activation(junk, src[:, 2 * i:2 * i + 2, :].rearrange("p k w -> p (k w)"), ACT.Square,
                                         accum_out=ssq[:, w, i:i + 1]).then_inc(sq_done, 1)
                act.wait_ge(norm_step, 5 * w + 1)
                nc.scalar.activation(wsc[:, w, 1:2], wsc[:, w, 0:1], ACT.Sqrt).then_inc(norm_sqrt, 1)

            def split(w):
                src = (v_raw if w == 0 else u_raw)
                act.wait_ge(norm_step, 5 * w + 5)
                for i in range(KT):
                    j = KT * w + i
                    if j >= 4:
                        act.wait_ge(split_copied, j - 3)
                    nc.scalar.activation(split_tmp[j % 4][:, 0:W], src[:, i, :], ACT.Copy, scale=wsc[:, w, 3:4])\
                        .then_inc(split_hi, 1)

            def pair(b):
                t0, t1 = tiles_of(b)
                if b == 0:
                    act.wait_ge(par_in, 16 * 7)
                    nc.scalar.activation(C_TG1, P_G1, ACT.Tanh).then_inc(tanh_ready, 1)
                    nc.scalar.activation(C_TG2, P_G2, ACT.Tanh).then_inc(tanh_ready, 1)
                    act.wait_ge(const_step, N_CONST)
                    quantise(t0)
                    chunks(range(0, CQ))
                    quantise(t1)
                    chunks(range(CQ, CB))
                else:
                    chunks(range(CB * b + 2 * CQ, CB * b + CB))
                sqrt2(t0)
                sqrt2(t1)

            def quantise(t):
                sqrt1(t)
                for j in range(3):
                    relu(t, j)
                centre(t, 0)
                centre(t, 1)
                relu(t, 3)
                centre(t, 2)
                centre(t, 3)

            def weights():
                act.wait_ge(v_in, 64)
                squares(0)
                split(0)
                for n in range(NQ):
                    for r in range(RT):
                        q = RT * n + r
                        act.wait_ge(ut_done, q + 1)
                        nc.scalar.activation(u_raw[:, q, :], yP[q % 2][:, :], ACT.Copy, scale=s_col[:, r:r + 1])\
                            .then_inc(ut_raw, 1)
                act.wait_ge(ut_raw, NQ * RT)
                squares(1)
                split(1)

            def stage2_block(u):
                q, t = u + 2 < NT, u + 2
                for p in range(NQ):
                    hi(x_piece(u, p), xT_hi[:, 4 * p:4 * p + 4, :].rearrange("p k w -> p (k w)"))
                if q:
                    sqrt1(t)
                h_out(u)
                hi(h_piece(u), hT_hi[:, :, :].rearrange("p k w -> p (k w)"))
                if q:
                    for j in range(3):
                        relu(t, j)
                    centre(t, 0)
                    centre(t, 1)
                if has_s1(u):
                    sqrt2(u + 1)
                if q:
                    relu(t, 3)
                    centre(t, 2)
                    centre(t, 3)
                bn = u // TB + 1
                if bn < NB and u % TB >= TB - 2:
                    n = u % TB - (TB - 2)
                    chunks(range(CB * bn + CQ * n, CB * bn + CQ * n + CQ))
                for hf in range(2):
                    act.wait_ge(y_ready, NQ * u + 2 * hf + 2)
                    act.dma_start(out_rows[u * P:(u + 1) * P, hf * D // 2:(hf + 1) * D // 2],
                                  ring[:, u % 3, hf * D // 2:(hf + 1) * D // 2]).then_inc(y_stored, 16)

            for b in range(NB):
                pair(b)
                if b == 0:
                    weights()
                for u in range(TB * b, TB * b + TB):
                    stage2_block(u)
            act.wait_ge(y_stored, 32 * NT)

        const_steps = [0]

        @block.vector
        def _(dve):
            ts, stt, tt = nc.vector.tensor_scalar, nc.vector.scalar_tensor_tensor, nc.vector.tensor_tensor

            def step(ins):
                const_steps[0] += 1
                ins.then_inc(const_step, 1)
                dve.wait_ge(const_step, const_steps[0])

            def constants():
                dve.wait_ge(par_in, 16 * 7)
                for s, r in ((P_S1, C_R1), (P_S2, C_R2)):
                    step(nc.vector.reciprocal(r, s))
                for z, c, mc, f in ((P_Z1, C_C1, C_MC1, C_F1), (P_Z2, C_C2, C_MC2, C_F2)):
                    step(ts(C_T0, z, 0.0, 255.0, ALU.max, ALU.min))
                    step(ts(mc, C_T0, MAGIC, None, ALU.add))
                    step(ts(c, mc, MAGIC, None, ALU.subtract))
                    step(tt(f, z, c, ALU.subtract))
                    step(ts(mc, mc, -1.0, None, ALU.mult))
                dve.wait_ge(tanh_ready, 2)
                step(stt(C_A, C_TG1, P_S1, P_S2, ALU.mult, ALU.mult))
                step(stt(C_AF1, C_A, -1.0, C_F1, ALU.mult, ALU.mult))
                step(stt(C_AF2, C_A, -1.0, C_F2, ALU.mult, ALU.mult))
                step(stt(C_AFF, C_AF1, -float(D), C_F2, ALU.mult, ALU.mult))

            def stats1(t):
                s = 6 * t
                dve.wait_ge(x_in, 16 * (t + 1))
                if t >= 1:
                    dve.wait_ge(q_relu, NQ * t)
                for n in range(NQ):
                    ins = nc.vector.bn_stats(st1[:, n, :], xq(t, n))
                ins.then_inc(ln1_step, 1)
                dve.wait_ge(ln1_step, s + 1)
                nc.vector.bn_aggr(ln1[:, 0:2], st1[:, :, :]).then_inc(ln1_agg, 1)
                dve.wait_ge(ln1_agg, t + 1)
                ts(ln1[:, 2:3], ln1[:, 1:2], EPS, None, ALU.add).then_inc(ln1_step, 1)
                dve.wait_ge(ln1_sqrt, t + 1)
                nc.vector.reciprocal(ln1[:, 4:5], ln1[:, 3:4]).then_inc(ln1_step, 1)
                dve.wait_ge(ln1_step, s + 3)
                stt(ln1[:, 7:8], ln1[:, 4:5], ln1[:, 2:3], ln1[:, 4:5], ALU.mult, ALU.mult).then_inc(ln1_step, 1)
                dve.wait_ge(ln1_step, s + 4)
                ts(ln1[:, 7:8], ln1[:, 7:8], -0.5, 1.5, ALU.mult, ALU.add).then_inc(ln1_agg2, 1)
                dve.wait_ge(ln1_agg2, 2 * t + 1)
                stt(ln1[:, 5:6], ln1[:, 4:5], C_R1, ln1[:, 7:8], ALU.mult, ALU.mult).then_inc(ln1_step, 1)
                dve.wait_ge(ln1_step, s + 5)
                stt(ln1[:, 7:8], ln1[:, 0:1], -1.0, ln1[:, 5:6], ALU.mult, ALU.mult).then_inc(ln1_agg2, 1)
                dve.wait_ge(ln1_agg2, 2 * t + 2)
                tt(ln1[:, 6:7], ln1[:, 7:8], P_Z1, ALU.add).then_inc(ln1_step, 1)

            def stats2(u):
                s, v = 6 * u, ln2[:, u % 2, :]
                dve.wait_ge(st2_ready, s1_unit(u, NQ - 1) + 1)
                nc.vector.bn_aggr(v[:, 0:2], st2[:, u % 2, :, :]).then_inc(ln2_step, 1)
                dve.wait_ge(ln2_step, s + 1)
                ts(v[:, 2:3], v[:, 1:2], EPS, None, ALU.add).then_inc(ln2_step, 1)
                dve.wait_ge(ln2_sqrt, u + 1)
                nc.vector.reciprocal(v[:, 4:5], v[:, 3:4]).then_inc(ln2_step, 1)
                dve.wait_ge(ln2_step, s + 3)
                stt(v[:, 7:8], v[:, 4:5], v[:, 2:3], v[:, 4:5], ALU.mult, ALU.mult).then_inc(ln2_step, 1)
                dve.wait_ge(ln2_step, s + 4)
                ts(v[:, 6:7], v[:, 7:8], -0.5, 1.5, ALU.mult, ALU.add).then_inc(ln2_step, 1)
                dve.wait_ge(ln2_step, s + 5)
                stt(v[:, 5:6], v[:, 4:5], XS, v[:, 6:7], ALU.mult, ALU.mult).then_inc(ln2_step, 1)

            def chunk(c):
                b, n, i = c // CB, c % CB // CQ, c % CQ
                a = stage[:, c % NST, :, :]
                dve.wait_ge(ctx_scaled, c + 1)
                ts(a, a, 255.0, MAGIC, ALU.min, ALU.add).then_inc(ctx_round, 1)
                dve.wait_ge(ctx_round, c + 1)
                if b > 0 and i == 0:
                    dve.wait_ge(s1_done, s1_unit(TB * b - 1, n) + 1)
                ts(q2[:, n, CK * i:CK * i + CK, :], a, C_MC2, None, ALU.add).then_inc(q2_ready, 1)

            def column_correction(b, n):
                dve.wait_ge(colsum_done, NQ * b + n + 1)
                ts(corr[:, n * W:(n + 1) * W], hP[:, :], C_AF1, C_AFF, ALU.mult, ALU.add).then_inc(corr_ready, 1)

            def row_correction(t):
                dve.wait_ge(q_ready, NQ * (t + 1))
                nc.vector.tensor_reduce(bvec[:, t % 2, 0:1], r1p[:, t % 2, :], AX.X, ALU.add).then_inc(row_step, 1)
                dve.wait_ge(row_step, 2 * t + 1)
                tt(bvec[:, t % 2, 1:2], bvec[:, t % 2, 0:1], C_AF2, ALU.mult).then_inc(row_step, 1)

            def x1_unit(t, n):
                i = s1_unit(t, n)
                dve.wait_ge(row_step, 2 * t + 2)
                dve.wait_ge(q_relu, NQ * (t + 1))
                dve.wait_ge(corr_ready, NQ * (t // TB) + n + 1)
                stt(xq(t, n), xq(t, n), bvec[:, t % 2, 1:2], corr[:, n * W:(n + 1) * W], ALU.add, ALU.add)\
                    .then_inc(xc_ready, 1)
                dve.wait_ge(xc_ready, i + 1)
                dve.wait_ge(s1_done, i + 1)
                stt(xq(t, n), acc[i % 2][:, :], C_A, xq(t, n), ALU.mult, ALU.add).then_inc(x1_ready, 1)
                dve.wait_ge(x1_ready, i + 1)
                nc.vector.bn_stats(st2[:, t % 2, n, :], xq(t, n)).then_inc(st2_ready, 1)

            def norm_piece(u, p):
                i = x_piece(u, p)
                if p == 0:
                    dve.wait_ge(ln2_step, 6 * u + 6)
                dve.wait_ge(t_written, i - 2)
                ts(piece[:, i % 3, :], xq(u, p), ln2[:, u % 2, 0:1], ln2[:, u % 2, 5:6], ALU.subtract, ALU.mult)\
                    .then_inc(xs_ready, 1)

            def lo(u, p):
                if p < NQ:
                    i, k = x_piece(u, p), slice(4 * p, 4 * p + 4)
                    h, l = xT_hi[:, k, :], xT_lo[:, k, :]
                else:
                    i, h, l = h_piece(u), hT_hi[:, :, :], hT_lo[:, :, :]
                flat = lambda a: a.rearrange("p k w -> p (k w)")
                dve.wait_ge(t_hi, 5 * u + p + 1)
                tt(flat(l), T[i % 3][:, :], flat(h), ALU.subtract).then_inc(t_read, 1)

            def round_piece(t, j):
                i = q_piece(t, j)
                dve.wait_ge(q_relu, NQ * t + j + 1)
                ts(piece[:, i % 3, :], piece[:, i % 3, :], 255.0, MAGIC, ALU.min, ALU.add).then_inc(q_round, 1)

            def qT_piece(t, j):
                i = q_piece(t, j)
                dve.wait_ge(t_written, i + 1)
                nc.vector.tensor_copy(qT[:, t % 2, 4 * j:4 * j + 4, :].rearrange("p k w -> p (k w)"),
                                      T[i % 3][:, 0:W // 2].bitcast(bf16)).then_inc(t_read, 1)

            def y_unit(u, n):
                i = NQ * u + n
                dve.wait_ge(y_done, i + 1)
                stt(xq(u, n), yP[i % 2][:, :], C_CY, xq(u, n), ALU.mult, ALU.add).then_inc(y_ready, 1)

            def quantise(t):
                stats1(t)
                for j in range(3):
                    round_piece(t, j)
                qT_piece(t, 0)
                round_piece(t, 3)
                for j in range(1, NQ):
                    qT_piece(t, j)
                row_correction(t)

            def pair(b):
                t0, t1 = tiles_of(b)
                if b == 0:
                    quantise(t0)
                    for c in range(CQ):
                        chunk(c)
                    quantise(t1)
                ahead = 1 if b == 0 else 2
                for n in range(NQ):
                    c = CB * b + CQ * (n + ahead)
                    more = n + ahead < NQ
                    if more:
                        for i in range(4):
                            chunk(c + i)
                    column_correction(b, n)
                    x1_unit(t0, n)
                    if more:
                        chunk(c + 4)
                        chunk(c + 5)
                    x1_unit(t1, n)
                    if more:
                        chunk(c + 6)
                        chunk(c + 7)
                stats2(t0)
                stats2(t1)

            def norm(w):
                s, v = 5 * w, wsc[:, w, :]
                dve.wait_ge(norm_sum, w + 1)
                nc.vector.tensor_reduce(v[:, 0:1], hP[:, 0:8], AX.X, ALU.add).then_inc(norm_step, 1)
                dve.wait_ge(norm_sqrt, w + 1)
                ts(v[:, 1:2], v[:, 1:2], 1e-30, None, ALU.max).then_inc(norm_step, 1)
                dve.wait_ge(norm_step, s + 2)
                ts(v[:, 2:3].bitcast(i32), v[:, 1:2].bitcast(i32), 0x7F800000, None, ALU.bitwise_and)\
                    .then_inc(norm_step, 1)
                dve.wait_ge(norm_step, s + 3)
                nc.vector.reciprocal(v[:, 3:4], v[:, 2:3]).then_inc(norm_step, 1)
                dve.wait_ge(norm_step, s + 4)
                ts(v[:, 3:4], v[:, 3:4], WS, None, ALU.mult).then_inc(norm_step, 1)
                dve.wait_ge(norm_step, s + 5)

            def split(w):
                src = (v_raw if w == 0 else u_raw)
                for i in range(KT):
                    j = KT * w + i
                    dve.wait_ge(split_hi, j + 1)
                    stt(split_tmp[j % 4][:, W:2 * W], src[:, i, :], wsc[:, w, 3:4], split_tmp[j % 4][:, 0:W],
                        ALU.mult, ALU.subtract).then_inc(split_lo, 1)

            def weights():
                norm(0)
                split(0)
                norm(1)
                split(1)
                stt(C_T0, wsc[:, 0, 2:3], 1.0 / (XS * HS * WS * WS), wsc[:, 1, 2:3], ALU.mult, ALU.mult)\
                    .then_inc(norm_step, 1)
                dve.wait_ge(norm_step, 11)
                tt(C_CY, C_T0, C_TG2, ALU.mult).then_inc(norm_step, 1)
                dve.wait_ge(norm_step, 12)

            def stage2_block(u):
                q, t = u + 2 < NT, u + 2
                bn = u // TB + 1
                more = bn < NB and u % TB >= TB - 2
                c = CB * bn + CQ * (u % TB - (TB - 2))
                for p in range(3):
                    norm_piece(u, p)
                for p in range(NQ):
                    if has_s1(u) and p < 3:
                        x1_unit(u + 1, p)
                    lo(u, p)
                    if p == 0:
                        norm_piece(u, 3)
                if q:
                    stats1(t)
                lo(u, NQ)
                if q:
                    for j in range(3):
                        round_piece(t, j)
                if has_s1(u):
                    x1_unit(u + 1, NQ - 1)
                    stats2(u + 1)
                for n in range(NQ):
                    y_unit(u, n)
                    if q and n < 2:
                        qT_piece(t, n)
                    if q and n == 0:
                        round_piece(t, 3)
                    if q and n == 2:
                        qT_piece(t, 2)
                        qT_piece(t, 3)
                    if more:
                        chunk(c + 2 * n)
                        chunk(c + 2 * n + 1)
                if q:
                    row_correction(t)

            constants()
            for b in range(NB):
                pair(b)
                if b == 0:
                    weights()
                for u in range(TB * b, TB * b + TB):
                    stage2_block(u)


_INS = ['x', 'ctx_4096', 'g_xattn', 'g_ffn', 'L0_xattn_x1_scale', 'L0_xattn_x1_zp', 'L0_xattn_x2_scale',
        'L0_xattn_x2_zp', 'L0_ffn_U', 'L0_ffn_S', 'L0_ffn_V']
_OUTS = [((2, 1024, 2048), 'float32')]


def kernel(**inputs):
    import numpy as _np
    import concourse.bacc as _bacc
    from concourse import mybir as _mybir
    from concourse.bass_utils import run_bass_kernel_spmd as _run

    nc = _bacc.Bacc("TRN2", target_bir_lowering=False, num_devices=1)
    arrays, args = {}, []
    for name in _INS:
        a = _np.ascontiguousarray(inputs[name])
        arrays[f"in_{name}_dram"] = a
        args.append(nc.dram_tensor(f"in_{name}_dram", a.shape, _mybir.dt.from_np(a.dtype), kind="ExternalInput").ap())
    for i, (shape, dtype) in enumerate(_OUTS):
        dt = _mybir.dt.from_np(_np.dtype(dtype))
        args.append(nc.dram_tensor(f"out_{i}_dram", shape, dt, kind="ExternalOutput").ap())
    gated_block_program(nc, *args)
    r = _run(nc, [arrays], core_ids=[0])
    return r.results[0]["out_0_dram"]
```

```python
import concourse.bass as bass
from concourse import mybir
from contextlib import ExitStack


def gated_block_program(nc, x, ctx_in, g_xattn, g_ffn, s1, z1, s2, z2, U, S, V, out):
    f32, bf16, f16, i32 = mybir.dt.float32, mybir.dt.bfloat16, mybir.dt.float16, mybir.dt.int32
    ALU, ACT, AX = mybir.AluOpType, mybir.ActivationFunctionType, mybir.AxisListType

    P = 128
    NB, SEQ, D = x.shape
    RANK = V.shape[1]
    KT = D // P
    RT = RANK // P
    W = 512
    NQ = D // W
    TB = SEQ // P
    NT = NB * TB
    CK = 2
    CQ = KT // CK
    CB = NQ * CQ
    NST = 4
    EPS = 1e-5
    MAGIC = 1.5 * 2.0 ** 23
    XS = 2.0 ** 9
    WS = 2.0 ** 14
    HS = 2.0 ** -15

    x_rows = x.rearrange("b s d -> (b s) d")
    out_rows = out.rearrange("b s d -> (b s) d")
    ctx_k = ctx_in.rearrange("b (k p) n -> b p k n", p=P)
    V_k = V.rearrange("(k p) r -> p k r", p=P)
    U_o = U.rearrange("(o p) r -> p o r", p=P)

    es = ExitStack()
    with es:
        def sb(name, shape, dt):
            return es.enter_context(nc.sbuf_tensor(name, shape, dt))

        def sem(name):
            return es.enter_context(nc.semaphore(name))

        q2 = sb("q2", [P, NQ, KT, W], bf16)
        v_hl = sb("v_hl", [P, KT, 2, W], f16)
        u_hl = sb("u_hl", [P, NQ, RT, 2, W], f16)
        ring = sb("ring", [P, 3, D], f32)
        qT = sb("qT", [P, 2, KT, P], bf16)
        xT_hi = sb("xT_hi", [P, KT, P], f16)
        xT_lo = sb("xT_lo", [P, KT, P], f16)
        piece = sb("piece", [P, 3, W], f32)
        qn = sb("qn", [P, 2, W], bf16)
        stage = sb("stage", [P, NST, CK, W], f32)
        hT_hi = sb("hT_hi", [P, RT, P], f16)
        hT_lo = sb("hT_lo", [P, RT, P], f16)
        corr = sb("corr", [P, D], f32)
        ident_f = sb("ident_f", [P, P], f32)
        ident_b = sb("ident_b", [P, P], bf16)
        ones_f = sb("ones_f", [P, P], f32)
        ones_b = sb("ones_b", [P, P], bf16)
        par = sb("par", [P, 6], f32)
        s_col = sb("s_col", [P, RT], f32)
        const = sb("const", [P, 24], f32)
        st1 = sb("st1", [P, NQ, 6], f32)
        st2 = sb("st2", [P, 2, NQ, 6], f32)
        ln1 = sb("ln1", [P, 8], f32)
        ln2 = sb("ln2", [P, 2, 8], f32)
        r1p = sb("r1p", [P, 2, NQ], f32)
        bvec = sb("bvec", [P, 2, 2], f32)
        ssq = sb("ssq", [P, 8 + 2 * NQ], f32)
        wsc = sb("wsc", [P, 1 + NQ, 5], f32)
        us_scale = sb("us_scale", [P, NQ, RT], f32)
        cy = sb("cy", [P, NQ], f32)

        def bank(name):
            return es.enter_context(nc.psum_tensor(name, [P, W], f32))

        acc = [bank("acc0"), bank("acc1")]
        hP = bank("hP")
        yP = [bank("y0"), bank("y1")]
        T = [bank("t0"), bank("t1"), bank("t2")]

        v_raw = u_hl[:, :, :, :, :].rearrange("p n r a w -> p (n r) (a w)").bitcast(f32)
        s_all = xT_hi[:, 0:2 * RT, :].rearrange("p k w -> p (k w)").bitcast(f32)
        junk = qn[:, :, :].rearrange("p a w -> p (a w)")

        (C_R1, C_R2, C_C1, C_C2, C_MC1, C_MC2, C_F1, C_F2, C_A, C_AF1, C_AF2, C_AFF, C_TG1, C_TG2,
         C_T0, C_SMAX, C_SMIN, C_TV) = [const[:, i:i + 1] for i in range(18)]
        P_S1, P_Z1, P_S2, P_Z2, P_G1, P_G2 = [par[:, i:i + 1] for i in range(6)]

        par_in = sem("par_in")
        x_in = sem("x_in")
        s_in = sem("s_in")
        stage_in = [sem(f"stage_in{i}") for i in range(NST)]
        v_in = sem("v_in")
        y_stored = sem("y_stored")
        setup_ready = sem("setup_ready")
        tanh_ready = sem("tanh_ready")
        const_step = sem("const_step")
        ctx_scaled = sem("ctx_scaled")
        ctx_round = sem("ctx_round")
        q2_ready = sem("q2_ready")
        colsum_done = sem("colsum_done")
        corr_ready = sem("corr_ready")
        ln1_step = sem("ln1_step")
        ln1_sqrt = sem("ln1_sqrt")
        ln1_agg = sem("ln1_agg")
        ln1_agg2 = sem("ln1_agg2")
        st2_ready = sem("st2_ready")
        ln2_step = sem("ln2_step")
        ln2_sqrt = sem("ln2_sqrt")
        q_relu = sem("q_relu")
        q_round = sem("q_round")
        q_ready = sem("q_ready")
        t_written = sem("t_written")
        t_read = sem("t_read")
        row_step = sem("row_step")
        xc_ready = sem("xc_ready")
        s1_done = sem("s1_done")
        x1_ready = sem("x1_ready")
        xs_ready = sem("xs_ready")
        t_hi = sem("t_hi")
        mm3_done = sem("mm3_done")
        h_evac = sem("h_evac")
        y_done = sem("y_done")
        y_ready = sem("y_ready")
        sq_done = sem("sq_done")
        norm_sum = sem("norm_sum")
        norm_step = sem("norm_step")
        norm_sqrt = sem("norm_sqrt")
        split_hi = sem("split_hi")
        split_lo = sem("split_lo")
        ut_done = sem("ut_done")

        def base(u):
            return 2 * NQ + (2 * NQ + 1) * u - (NQ if u == NT - 1 else 0)

        def x_piece(u, p):
            return base(u) + p

        def h_piece(u):
            return base(u) + NQ

        def q_piece(t, j):
            return NQ * t + j if t < 2 else base(t - 2) + NQ + 1 + j

        def s1_unit(t, n):
            b, m = t // TB, t % TB
            return NQ * TB * b + (2 * n + m if m < 2 else NQ * m + n)

        def stage_count(c):
            extra = (D // P // CK) // NST if c >= CB else 0
            return 16 * (c // NST + 1 + extra)

        NU = D // P // CK
        N_CONST = 16
        NORM_STEPS = 7

        def boundary_chunks(u):
            b, n = u // TB + 1, u % TB - (TB - 2)
            return list(range(CB * b + CQ * n, CB * b + CQ * (n + 1))) if b < NB and n >= 0 else []
        has_s1 = lambda u: u % TB not in (0, TB - 1)
        has_last = lambda u: u % TB != TB - 1

        def unit_bank(t, n):
            m = t % TB
            return (yP, acc)[n % 2][m] if m < 2 else acc[s1_unit(t, n) % 2]

        def colsum_bank(b, n):
            return acc[0] if b > 0 and n == 0 else hP
        xq = lambda t, n: ring[:, t % 3, n * W:(n + 1) * W]
        tiles_of = lambda b: (TB * b, TB * b + 1)

        block = es.enter_context(nc.Block())

        @block.gpsimd
        def _(pool):
            nc.gpsimd.memset(ident_f[:, :], 0.0)
            nc.gpsimd.memset(ident_b[:, :], 0.0)
            nc.gpsimd.memset(ones_f[:, :], 1.0)
            nc.gpsimd.memset(ones_b[:, :], 1.0).then_inc(setup_ready, 1)
            pool.wait_ge(setup_ready, 1)
            for m in (ident_f, ident_b):
                nc.gpsimd.affine_select(out=m[:, :], in_=m[:, :], compare_op=ALU.not_equal, fill=1.0,
                                        base=0, pattern=[[-1, P]], channel_multiplier=1)\
                    .then_inc(setup_ready, 1)

        @block.sync
        def _(sp):
            def load_x(t):
                if t >= 3:
                    sp.wait_ge(y_stored, 32 * (t - 2))
                if t >= 1:
                    sp.wait_ge(x_in, 16 * t)
                sp.dma_start(ring[:, t % 3, :], x_rows[t * P:(t + 1) * P, :]).then_inc(x_in, 16)

            def load_chunks(b, n, first=0, end=CQ):
                for i in range(first, end):
                    c = CB * b + CQ * n + i
                    if NST <= c < CB or c >= CB + NST:
                        sp.wait_ge(q2_ready, c - NST + 1)
                    elif c >= CB:
                        sp.wait_ge(ut_done, NQ * RT)
                    sp.dma_start(stage[:, c % NST, :, :],
                                 ctx_k[b, :, CK * i:CK * i + CK, n * W:(n + 1) * W])\
                        .then_inc(stage_in[c % NST], 16)

            for i, a in enumerate((s1, z1, s2, z2, g_xattn, g_ffn)):
                with nc.allow_non_contiguous_dma(reason="one scalar to all partitions"):
                    sp.dma_start(par[:, i:i + 1], a.rearrange("(o a) -> o a", o=1).to_broadcast([P, 1]))\
                        .then_inc(par_in, 16)
            with nc.allow_non_contiguous_dma(reason="512 scales"):
                sp.dma_start(s_col[:, :], S.rearrange("(r p) -> p r", p=P)).then_inc(par_in, 16)
            load_x(0)
            load_chunks(0, 0)
            load_x(1)
            load_chunks(0, 1)
            for i in range(4):
                sp.dma_start(v_raw[:, 4 * i:4 * i + 4, :], V_k[:, 4 * i:4 * i + 4, :]).then_inc(v_in, 16)
            sp.dma_start(s_all, S.rearrange("(o a) -> o a", o=1).to_broadcast([P, RANK])).then_inc(s_in, 16)
            load_chunks(0, 2)
            load_chunks(0, 3)
            load_x(2)
            for i in range(NU):
                if i < NST:
                    sp.wait_ge(q2_ready, CB - NST + i + 1)
                else:
                    sp.wait_ge(ut_done, RT * ((i - NST) // 2 + 1))
                sp.dma_start(stage[:, i % NST, :, :], U_o[:, CK * i:CK * i + CK, :])\
                    .then_inc(stage_in[i % NST], 16)
            for u in range(NT - 3):
                if u % TB == TB - 2:
                    load_chunks(u // TB + 1, 0)
                    load_chunks(u // TB + 1, 1, 0, NST)
                if u % TB == TB - 1:
                    load_chunks(u // TB + 1, 1, NST, CQ)
                    for n in range(2, NQ):
                        load_chunks(u // TB + 1, n)
                load_x(u + 3)

        @block.tensor
        def _(pe):
            def q_transpose(t, j):
                i = q_piece(t, j)
                pe.wait_ge(q_ready, NQ * t + j + 1)
                if i >= 3:
                    pe.wait_ge(t_read, i - 2)
                dst = T[i % 3][:, 0:W // 2].bitcast(bf16)
                for k in range(4):
                    mm = nc.tensor.transpose(dst[:, k * P:(k + 1) * P], qn[:, j % 2, k * P:(k + 1) * P], ident_b[:, :])
                mm.then_inc(t_written, 1)

            def f_transpose(i):
                pe.wait_ge(t_read, i - 2)
                for k in range(4):
                    mm = nc.tensor.transpose(T[i % 3][:, k * P:(k + 1) * P], piece[:, i % 3, k * P:(k + 1) * P],
                                             ident_f[:, :])
                mm.then_inc(t_written, 1)

            def x_transpose(u, p):
                pe.wait_ge(xs_ready, NQ * u + p + 1)
                f_transpose(x_piece(u, p))

            def colsum(b, n, k0=0, k1=KT):
                if k0 == 0 and b > 0 and n == 0:
                    pe.wait_ge(x1_ready, NQ * TB * b)
                if k0 == 0 and b > 0 and n == 1:
                    pe.wait_ge(h_evac, TB * b)
                if k0 == 0 and n > 0:
                    pe.wait_ge(corr_ready, NQ * b + n)
                for k in range(k0, k1):
                    if k % CK == 0:
                        pe.wait_ge(q2_ready, CB * b + CQ * n + k // CK + 1)
                    mm = nc.tensor.matmul(colsum_bank(b, n)[:, :], ones_b[:, :], q2[:, n, k, :],
                                          start=(k == 0), stop=(k == KT - 1))
                if k1 == KT:
                    mm.then_inc(colsum_done, 1)

            def s1_part(t, n, k0, k1):
                i, b, m = s1_unit(t, n), t // TB, t % TB
                if k0 == 0:
                    pe.wait_ge(t_read, q_piece(t, NQ - 1) + 1)
                    if m >= 2:
                        pe.wait_ge(x1_ready, i - 1)
                    elif n >= 2:
                        pe.wait_ge(x1_ready, s1_unit(t, n - 2) + 1)
                    elif b > 0 and n == 0:
                        pe.wait_ge(y_ready, NQ * TB * b)
                    elif b > 0:
                        pe.wait_ge(x1_ready, NQ * TB * b)
                        pe.wait_ge(corr_ready, NQ * b + 1)
                    if i == 8:
                        pe.wait_ge(split_lo, 2 * KT)
                for k in range(k0, k1):
                    mm = nc.tensor.matmul(unit_bank(t, n)[:, :], qT[:, t % 2, k, :], q2[:, n, k, :],
                                          start=(k == 0), stop=(k == KT - 1))
                if k1 == KT:
                    mm.then_inc(s1_done, 1)

            def mm3(u, k0=0, k1=KT):
                if k0 == 0:
                    pe.wait_ge(corr_ready, NQ * (u // TB + 1))
                    if u == 0:
                        pe.wait_ge(split_lo, KT)
                    else:
                        pe.wait_ge(h_evac, u)
                for k in range(k0, k1):
                    if k % 4 == 0:
                        pe.wait_ge(t_read, x_piece(u, k // 4) + 1)
                    nc.tensor.matmul(hP[:, :], xT_hi[:, k, :], v_hl[:, k, 0, :], start=(k == 0), stop=False)
                    nc.tensor.matmul(hP[:, :], xT_hi[:, k, :], v_hl[:, k, 1, :], start=False, stop=False)
                    mm = nc.tensor.matmul(hP[:, :], xT_lo[:, k, :], v_hl[:, k, 0, :], start=False, stop=(k == KT - 1))
                if k1 == KT:
                    mm.then_inc(mm3_done, 1)

            def mm4(u, n):
                i = NQ * u + n
                if n == 0:
                    pe.wait_ge(t_read, h_piece(u) + 1)
                if u % TB == 0 and n < 2:
                    pe.wait_ge(x1_ready, s1_unit(u + 1, 2) + 1)
                if u == 0:
                    pe.wait_ge(split_lo, KT + RT * NQ if n < 2 else KT + RT * (n + 1))
                if i >= 2:
                    pe.wait_ge(y_ready, i - 1)
                for r in range(RT):
                    nc.tensor.matmul(yP[i % 2][:, :], hT_hi[:, r, :], u_hl[:, n, r, 0, :], start=(r == 0), stop=False)
                    nc.tensor.matmul(yP[i % 2][:, :], hT_hi[:, r, :], u_hl[:, n, r, 1, :], start=False, stop=False)
                    mm = nc.tensor.matmul(yP[i % 2][:, :], hT_lo[:, r, :], u_hl[:, n, r, 0, :],
                                          start=False, stop=(r == RT - 1))
                mm.then_inc(y_done, 1)

            def pair(b):
                t0, t1 = tiles_of(b)
                if b == 0:
                    pe.wait_ge(setup_ready, 3)
                    for j in range(NQ):
                        q_transpose(t0, j)
                for n in range(NQ):
                    if b == 0 or n > 0:
                        colsum(b, n)
                    if b == 0 and n == 2:
                        pe.wait_ge(sq_done, 8)
                        nc.tensor.matmul(T[2][:, 0:8], ones_f[:, :], ssq[:, 0:8], start=True, stop=True)\
                            .then_inc(norm_sum, 1)
                    s1_part(t0, n, 0, KT)
                    if b == 0 and n == 0:
                        for j in range(NQ):
                            q_transpose(t1, j)
                    if n < NQ - 1:
                        s1_part(t1, n, 0, KT)

            def u_norm(n):
                pe.wait_ge(sq_done, 8 + 2 * n + 2)
                if n == 0:
                    pe.wait_ge(x1_ready, s1_unit(0, NQ - 1) + 1)
                    pe.wait_ge(x1_ready, s1_unit(1, 2) + 1)
                else:
                    pe.wait_ge(norm_step, NORM_STEPS * n + 1)
                nc.tensor.matmul(acc[0][:, 0:2], ones_f[:, :], ssq[:, 8 + 2 * n:10 + 2 * n], start=True, stop=True)\
                    .then_inc(norm_sum, 1)

            def u_transpose(n, rs):
                for r in rs:
                    q = RT * n + r
                    if q >= 2:
                        pe.wait_ge(split_lo, KT + q - 1)
                    for k in range(4):
                        i = 2 * n + k // 2
                        mm = nc.tensor.transpose(yP[q % 2][:, k * P:(k + 1) * P],
                                                 stage[:, i % NST, k % 2, r * P:(r + 1) * P], ident_f[:, :])
                    mm.then_inc(ut_done, 1)

            def stage2_block(u):
                t = u + 1
                if has_s1(u):
                    for n in range(NQ - 1):
                        s1_part(t, n, 0, KT)
                        x_transpose(u, n)
                    x_transpose(u, NQ - 1)
                else:
                    if u == 0:
                        pe.wait_ge(norm_step, 1)
                    for p in range(NQ):
                        x_transpose(u, p)
                if u == 0:
                    u_norm(0)
                    for n in range(NQ):
                        u_transpose(n, (0, 1))
                        mm3(u, 4 * n, 4 * n + 2)
                        if n + 1 < NQ:
                            u_norm(n + 1)
                        u_transpose(n, (2, 3))
                        mm3(u, 4 * n + 2, 4 * n + 4)
                else:
                    mm3(u)
                fill = None
                if has_last(u):
                    fill = lambda k0, k1: s1_part(t, NQ - 1, k0, k1)
                elif u + 1 < NT:
                    fill = lambda k0, k1: colsum(u // TB + 1, 0, k0, k1)
                if fill:
                    fill(0, KT // 2)
                pe.wait_ge(h_evac, u + 1)
                f_transpose(h_piece(u))
                if fill:
                    fill(KT // 2, KT)
                q = u + 2 < NT
                for n in range(NQ):
                    mm4(u, n)
                    if q and n < 2:
                        q_transpose(u + 2, n)
                    if q and n == 2:
                        q_transpose(u + 2, 2)
                        q_transpose(u + 2, 3)

            for b in range(NB):
                pair(b)
                for u in range(TB * b, TB * b + TB):
                    stage2_block(u)

        @block.scalar
        def _(act):
            def chunks(cs):
                for c in cs:
                    act.wait_ge(stage_in[c % NST], stage_count(c))
                    a = stage[:, c % NST, :, :]
                    nc.scalar.activation(a, a, ACT.Relu, bias=P_Z2, scale=C_R2).then_inc(ctx_scaled, 1)

            def sqrt1(t):
                act.wait_ge(ln1_step, 6 * t + 2)
                nc.scalar.activation(ln1[:, 3:4], ln1[:, 2:3], ACT.Sqrt).then_inc(ln1_sqrt, 1)

            def sqrt2(u):
                act.wait_ge(ln2_step, 6 * u + 2)
                nc.scalar.activation(ln2[:, u % 2, 3:4], ln2[:, u % 2, 2:3], ACT.Sqrt).then_inc(ln2_sqrt, 1)

            def relu(t, j):
                i = q_piece(t, j)
                act.wait_ge(ln1_step, 6 * t + 6)
                if i >= 3:
                    act.wait_ge(t_written, i - 2)
                nc.scalar.activation(piece[:, i % 3, :], xq(t, j), ACT.Relu, bias=ln1[:, 6:7], scale=ln1[:, 5:6])\
                    .then_inc(q_relu, 1)

            def centre(t, j):
                i = q_piece(t, j)
                act.wait_ge(q_round, NQ * t + j + 1)
                if NQ * t + j >= 2:
                    ip = q_piece(t, j - 2) if j >= 2 else q_piece(t - 1, j + 2)
                    act.wait_ge(t_written, ip + 1)
                if t >= 2:
                    act.wait_ge(row_step, 2 * (t - 1))
                if t == 2 and j < 2:
                    act.wait_ge(sq_done, 8 + 2 * NQ)
                nc.scalar.activation(qn[:, j % 2, :], piece[:, i % 3, :], ACT.Identity, bias=C_MC1,
                                     accum_out=r1p[:, t % 2, j:j + 1]).then_inc(q_ready, 1)

            def hi(i, dst):
                act.wait_ge(t_written, i + 1)
                nc.scalar.activation(dst, T[i % 3][:, :], ACT.Copy).then_inc(t_hi, 1)

            def h_out(u):
                i = h_piece(u)
                act.wait_ge(mm3_done, u + 1)
                act.wait_ge(t_written, i - 2)
                nc.scalar.activation(piece[:, i % 3, :], hP[:, :], ACT.Copy, scale=HS).then_inc(h_evac, 1)

            def square(i, src):
                if i:
                    act.wait_ge(sq_done, i)
                nc.scalar.activation(junk, src.rearrange("p k w -> p (k w)"), ACT.Square, accum_out=ssq[:, i:i + 1])\
                    .then_inc(sq_done, 1)

            def norm_root(w):
                act.wait_ge(norm_step, NORM_STEPS * w + 1)
                nc.scalar.activation(wsc[:, w, 1:2], wsc[:, w, 0:1], ACT.Sqrt).then_inc(norm_sqrt, 1)

            def v_high(i):
                act.wait_ge(norm_step, NORM_STEPS)
                nc.scalar.activation(v_hl[:, i, 0, :], v_raw[:, i, :], ACT.Copy, scale=wsc[:, 0, 3:4])\
                    .then_inc(split_hi, 1)

            def u_squares(n):
                for i in (2 * n, 2 * n + 1):
                    act.wait_ge(stage_in[i % NST], 16 * (CB // NST + i // NST + 1))
                    square(8 + i, stage[:, i % NST, :, :])

            def u_high(n):
                act.wait_ge(norm_step, NORM_STEPS * (n + 2))
                for r in range(RT):
                    q = RT * n + r
                    act.wait_ge(split_lo, KT)
                    act.wait_ge(ut_done, q + 1)
                    nc.scalar.activation(u_hl[:, n, r, 0, :], yP[q % 2][:, :], ACT.Copy, scale=us_scale[:, n, r:r + 1])\
                        .then_inc(split_hi, 1)

            def pair(b):
                t0, t1 = tiles_of(b)
                if b == 0:
                    act.wait_ge(par_in, 16 * 7)
                    nc.scalar.activation(C_TG1, P_G1, ACT.Tanh).then_inc(tanh_ready, 1)
                    nc.scalar.activation(C_TG2, P_G2, ACT.Tanh).then_inc(tanh_ready, 1)
                    act.wait_ge(const_step, N_CONST)
                    quantise(t0, range(0, CQ))
                    quantise(t1, range(CQ, 2 * CQ))
                    act.wait_ge(v_in, 64)
                    act.wait_ge(t_written, q_piece(t1, NQ - 1) + 1)
                    for i in range(CQ):
                        chunks([2 * CQ + i])
                        square(i, v_raw[:, 2 * i:2 * i + 2, :])
                    chunks([3 * CQ, 3 * CQ + 1])
                    norm_root(0)
                    for i in range(2, CQ):
                        v_high(2 * i - 4)
                        v_high(2 * i - 3)
                        chunks([3 * CQ + i])
                    for i in range(2 * CQ - 4, KT):
                        v_high(i)
                else:
                    chunks(range(CB * b + 2 * CQ, CB * b + CB))
                sqrt2(t0)

            def quantise(t, cs):
                chunks(cs[0:2])
                sqrt1(t)
                chunks(cs[2:3])
                for j in range(3):
                    relu(t, j)
                chunks(cs[3:4])
                centre(t, 0)
                centre(t, 1)
                chunks(cs[4:5])
                relu(t, 3)
                centre(t, 2)
                chunks(cs[5:6])
                centre(t, 3)
                chunks(cs[6:8])

            def stage2_block(u):
                q, t = u + 2 < NT, u + 2
                for p in range(NQ):
                    hi(x_piece(u, p), xT_hi[:, 4 * p:4 * p + 4, :].rearrange("p k w -> p (k w)"))
                if u == 0:
                    u_squares(0)
                    norm_root(1)
                    for n in range(NQ):
                        if n + 1 < NQ:
                            u_squares(n + 1)
                        u_high(n)
                        if n + 1 < NQ:
                            norm_root(n + 2)
                if q:
                    sqrt1(t)
                chunks(boundary_chunks(u)[:5])
                h_out(u)
                hi(h_piece(u), hT_hi[:, :, :].rearrange("p k w -> p (k w)"))
                if q:
                    for j in range(3):
                        relu(t, j)
                    centre(t, 0)
                    centre(t, 1)
                if has_last(u):
                    sqrt2(u + 1)
                if q:
                    relu(t, 3)
                    centre(t, 2)
                    centre(t, 3)
                chunks(boundary_chunks(u)[5:])
                for hf in range(2):
                    act.wait_ge(y_ready, NQ * u + 2 * hf + 2)
                    act.dma_start(out_rows[u * P:(u + 1) * P, hf * D // 2:(hf + 1) * D // 2],
                                  ring[:, u % 3, hf * D // 2:(hf + 1) * D // 2]).then_inc(y_stored, 16)

            for b in range(NB):
                pair(b)
                for u in range(TB * b, TB * b + TB):
                    stage2_block(u)
            act.wait_ge(y_stored, 32 * NT)

        const_steps = [0]

        @block.vector
        def _(dve):
            ts, stt, tt = nc.vector.tensor_scalar, nc.vector.scalar_tensor_tensor, nc.vector.tensor_tensor

            def step(ins):
                const_steps[0] += 1
                ins.then_inc(const_step, 1)
                dve.wait_ge(const_step, const_steps[0])

            def constants():
                dve.wait_ge(par_in, 16 * 7)
                for s, r in ((P_S1, C_R1), (P_S2, C_R2)):
                    step(nc.vector.reciprocal(r, s))
                for z, c, mc, f in ((P_Z1, C_C1, C_MC1, C_F1), (P_Z2, C_C2, C_MC2, C_F2)):
                    step(ts(C_T0, z, 0.0, 255.0, ALU.max, ALU.min))
                    step(ts(mc, C_T0, MAGIC, None, ALU.add))
                    step(ts(c, mc, MAGIC, None, ALU.subtract))
                    step(tt(f, z, c, ALU.subtract))
                    step(ts(mc, mc, -1.0, None, ALU.mult))
                dve.wait_ge(tanh_ready, 2)
                step(stt(C_A, C_TG1, P_S1, P_S2, ALU.mult, ALU.mult))
                step(stt(C_AF1, C_A, -1.0, C_F1, ALU.mult, ALU.mult))
                step(stt(C_AF2, C_A, -1.0, C_F2, ALU.mult, ALU.mult))
                step(stt(C_AFF, C_AF1, -float(D), C_F2, ALU.mult, ALU.mult))

            def largest_s():
                dve.wait_ge(s_in, 16)
                step(nc.vector.tensor_reduce(C_SMAX, s_all, AX.X, ALU.max))
                step(nc.vector.tensor_reduce(C_SMIN, s_all, AX.X, ALU.min))
                step(stt(C_SMAX, C_SMIN, -1.0, C_SMAX, ALU.mult, ALU.max))

            def stats1(t):
                s = 6 * t
                dve.wait_ge(x_in, 16 * (t + 1))
                if t >= 1:
                    dve.wait_ge(q_relu, NQ * t)
                for n in range(NQ):
                    ins = nc.vector.bn_stats(st1[:, n, :], xq(t, n))
                ins.then_inc(ln1_step, 1)
                dve.wait_ge(ln1_step, s + 1)
                nc.vector.bn_aggr(ln1[:, 0:2], st1[:, :, :]).then_inc(ln1_agg, 1)
                dve.wait_ge(ln1_agg, t + 1)
                ts(ln1[:, 2:3], ln1[:, 1:2], EPS, None, ALU.add).then_inc(ln1_step, 1)
                dve.wait_ge(ln1_sqrt, t + 1)
                nc.vector.reciprocal(ln1[:, 4:5], ln1[:, 3:4]).then_inc(ln1_step, 1)
                dve.wait_ge(ln1_step, s + 3)
                stt(ln1[:, 7:8], ln1[:, 4:5], ln1[:, 2:3], ln1[:, 4:5], ALU.mult, ALU.mult).then_inc(ln1_step, 1)
                dve.wait_ge(ln1_step, s + 4)
                ts(ln1[:, 7:8], ln1[:, 7:8], -0.5, 1.5, ALU.mult, ALU.add).then_inc(ln1_agg2, 1)
                dve.wait_ge(ln1_agg2, 2 * t + 1)
                stt(ln1[:, 5:6], ln1[:, 4:5], C_R1, ln1[:, 7:8], ALU.mult, ALU.mult).then_inc(ln1_step, 1)
                dve.wait_ge(ln1_step, s + 5)
                stt(ln1[:, 7:8], ln1[:, 0:1], -1.0, ln1[:, 5:6], ALU.mult, ALU.mult).then_inc(ln1_agg2, 1)
                dve.wait_ge(ln1_agg2, 2 * t + 2)
                tt(ln1[:, 6:7], ln1[:, 7:8], P_Z1, ALU.add).then_inc(ln1_step, 1)

            def stats2(u):
                s, v = 6 * u, ln2[:, u % 2, :]
                dve.wait_ge(st2_ready, s1_unit(u, NQ - 1) + 1)
                nc.vector.bn_aggr(v[:, 0:2], st2[:, u % 2, :, :]).then_inc(ln2_step, 1)
                dve.wait_ge(ln2_step, s + 1)
                ts(v[:, 2:3], v[:, 1:2], EPS, None, ALU.add).then_inc(ln2_step, 1)
                dve.wait_ge(ln2_sqrt, u + 1)
                nc.vector.reciprocal(v[:, 4:5], v[:, 3:4]).then_inc(ln2_step, 1)
                dve.wait_ge(ln2_step, s + 3)
                stt(v[:, 7:8], v[:, 4:5], v[:, 2:3], v[:, 4:5], ALU.mult, ALU.mult).then_inc(ln2_step, 1)
                dve.wait_ge(ln2_step, s + 4)
                ts(v[:, 6:7], v[:, 7:8], -0.5, 1.5, ALU.mult, ALU.add).then_inc(ln2_step, 1)
                dve.wait_ge(ln2_step, s + 5)
                stt(v[:, 5:6], v[:, 4:5], XS, v[:, 6:7], ALU.mult, ALU.mult).then_inc(ln2_step, 1)

            def chunk(c):
                b, n, i = c // CB, c % CB // CQ, c % CQ
                a = stage[:, c % NST, :, :]
                dve.wait_ge(ctx_scaled, c + 1)
                ts(a, a, 255.0, MAGIC, ALU.min, ALU.add).then_inc(ctx_round, 1)
                dve.wait_ge(ctx_round, c + 1)
                if b > 0 and i == 0:
                    dve.wait_ge(s1_done, s1_unit(TB * b - 1, n) + 1)
                ts(q2[:, n, CK * i:CK * i + CK, :], a, C_MC2, None, ALU.add).then_inc(q2_ready, 1)

            def column_correction(b, n):
                dve.wait_ge(colsum_done, NQ * b + n + 1)
                ts(corr[:, n * W:(n + 1) * W], colsum_bank(b, n)[:, :], C_AF1, C_AFF, ALU.mult, ALU.add).then_inc(corr_ready, 1)

            def row_correction(t):
                dve.wait_ge(q_ready, NQ * (t + 1))
                nc.vector.tensor_reduce(bvec[:, t % 2, 0:1], r1p[:, t % 2, :], AX.X, ALU.add).then_inc(row_step, 1)
                dve.wait_ge(row_step, 2 * t + 1)
                tt(bvec[:, t % 2, 1:2], bvec[:, t % 2, 0:1], C_AF2, ALU.mult).then_inc(row_step, 1)

            def x1_unit(t, n):
                i = s1_unit(t, n)
                dve.wait_ge(row_step, 2 * t + 2)
                dve.wait_ge(q_relu, NQ * (t + 1))
                dve.wait_ge(corr_ready, NQ * (t // TB) + n + 1)
                stt(xq(t, n), xq(t, n), bvec[:, t % 2, 1:2], corr[:, n * W:(n + 1) * W], ALU.add, ALU.add)\
                    .then_inc(xc_ready, 1)
                dve.wait_ge(xc_ready, i + 1)
                dve.wait_ge(s1_done, i + 1)
                stt(xq(t, n), unit_bank(t, n)[:, :], C_A, xq(t, n), ALU.mult, ALU.add).then_inc(x1_ready, 1)
                dve.wait_ge(x1_ready, i + 1)
                nc.vector.bn_stats(st2[:, t % 2, n, :], xq(t, n)).then_inc(st2_ready, 1)

            def norm_piece(u, p):
                i = x_piece(u, p)
                if p == 0:
                    dve.wait_ge(ln2_step, 6 * u + 6)
                dve.wait_ge(t_written, i - 2)
                ts(piece[:, i % 3, :], xq(u, p), ln2[:, u % 2, 0:1], ln2[:, u % 2, 5:6], ALU.subtract, ALU.mult)\
                    .then_inc(xs_ready, 1)

            def lo(u, p):
                if p < NQ:
                    i, k = x_piece(u, p), slice(4 * p, 4 * p + 4)
                    h, l = xT_hi[:, k, :], xT_lo[:, k, :]
                else:
                    i, h, l = h_piece(u), hT_hi[:, :, :], hT_lo[:, :, :]
                flat = lambda a: a.rearrange("p k w -> p (k w)")
                dve.wait_ge(t_hi, 5 * u + p + 1)
                tt(flat(l), T[i % 3][:, :], flat(h), ALU.subtract).then_inc(t_read, 1)

            def round_piece(t, j):
                i = q_piece(t, j)
                dve.wait_ge(q_relu, NQ * t + j + 1)
                ts(piece[:, i % 3, :], piece[:, i % 3, :], 255.0, MAGIC, ALU.min, ALU.add).then_inc(q_round, 1)

            def qT_piece(t, j):
                i = q_piece(t, j)
                dve.wait_ge(t_written, i + 1)
                nc.vector.tensor_copy(qT[:, t % 2, 4 * j:4 * j + 4, :].rearrange("p k w -> p (k w)"),
                                      T[i % 3][:, 0:W // 2].bitcast(bf16)).then_inc(t_read, 1)

            def y_unit(u, n):
                i = NQ * u + n
                dve.wait_ge(y_done, i + 1)
                stt(xq(u, n), yP[i % 2][:, :], cy[:, n:n + 1], xq(u, n), ALU.mult, ALU.add).then_inc(y_ready, 1)

            def quantise(t, cs):
                stats1(t)
                chunk(cs[0])
                if t > 0:
                    column_correction(0, 0)
                chunk(cs[1])
                chunk(cs[2])
                for j in range(3):
                    round_piece(t, j)
                chunk(cs[3])
                qT_piece(t, 0)
                chunk(cs[4])
                round_piece(t, 3)
                qT_piece(t, 1)
                qT_piece(t, 2)
                chunk(cs[5])
                qT_piece(t, 3)
                row_correction(t)
                chunk(cs[6])
                chunk(cs[7])

            def pair(b):
                t0, t1 = tiles_of(b)
                if b == 0:
                    quantise(t0, range(0, CQ))
                    quantise(t1, range(CQ, 2 * CQ))
                ahead = 1 if b == 0 else 2
                for n in range(NQ):
                    for i in range(CQ):
                        if b == 0 and n == 1 and i == 4:
                            largest_s()
                        if b == 0 and n == 2 and i == 2:
                            v_norm()
                        if b == 0 and n == 2 and i >= 2:
                            v_low(2 * i - 4)
                            v_low(2 * i - 3)
                        if n + ahead < NQ and (b, n) != (0, 0):
                            chunk(CB * b + CQ * (n + ahead) + i)
                        if i == 1 and n > 0:
                            column_correction(b, n)
                    if b == 0 and n == 2:
                        for i in range(2 * CQ - 4, KT):
                            v_low(i)
                    x1_unit(t0, n)
                    if n < NQ - 1:
                        x1_unit(t1, n)
                stats2(t0)

            def norm(w, sums, factor):
                s, v = NORM_STEPS * w, wsc[:, w, :]
                dve.wait_ge(norm_sum, w + 1)
                nc.vector.tensor_reduce(v[:, 0:1], sums, AX.X, ALU.add).then_inc(norm_step, 1)
                dve.wait_ge(norm_sqrt, w + 1)
                ts(v[:, 1:2], v[:, 1:2], factor, 1e-30, ALU.mult, ALU.max).then_inc(norm_step, 1)
                dve.wait_ge(norm_step, s + 2)
                ts(v[:, 2:3].bitcast(i32), v[:, 1:2].bitcast(i32), 0x7F800000, None, ALU.bitwise_and)\
                    .then_inc(norm_step, 1)
                dve.wait_ge(norm_step, s + 3)
                nc.vector.reciprocal(v[:, 3:4], v[:, 2:3]).then_inc(norm_step, 1)
                dve.wait_ge(norm_step, s + 4)
                ts(v[:, 3:4], v[:, 3:4], WS, None, ALU.mult).then_inc(norm_step, 1)
                dve.wait_ge(norm_step, s + 5)

            def v_norm():
                norm(0, T[2][:, 0:8], 1.0)
                ts(C_TV, wsc[:, 0, 2:3], 1.0 / (XS * HS * WS * WS), None, ALU.mult).then_inc(norm_step, 1)
                dve.wait_ge(norm_step, NORM_STEPS - 1)
                tt(C_TV, C_TV, C_TG2, ALU.mult).then_inc(norm_step, 1)
                dve.wait_ge(norm_step, NORM_STEPS)

            def v_low(i):
                dve.wait_ge(split_hi, i + 1)
                stt(v_hl[:, i, 1, :], v_raw[:, i, :], wsc[:, 0, 3:4], v_hl[:, i, 0, :], ALU.mult, ALU.subtract)\
                    .then_inc(split_lo, 1)

            def u_norm(n):
                w = n + 1
                norm(w, acc[0][:, 0:2], C_SMAX)
                tt(cy[:, n:n + 1], wsc[:, w, 2:3], C_TV, ALU.mult).then_inc(norm_step, 1)
                ts(us_scale[:, n, :], s_col[:, :], wsc[:, w, 3:4], None, ALU.mult).then_inc(norm_step, 1)
                dve.wait_ge(norm_step, NORM_STEPS * (w + 1))

            def u_low(n):
                for r in range(RT):
                    q = RT * n + r
                    dve.wait_ge(split_hi, KT + q + 1)
                    stt(u_hl[:, n, r, 1, :], yP[q % 2][:, :], us_scale[:, n, r:r + 1], u_hl[:, n, r, 0, :],
                        ALU.mult, ALU.subtract).then_inc(split_lo, 1)

            def stage2_block(u):
                q, t = u + 2 < NT, u + 2
                cs = boundary_chunks(u)
                if u % TB == 0:
                    for p in range(3):
                        norm_piece(u, p)
                for p in range(NQ):
                    if has_s1(u) and p < 3:
                        x1_unit(u + 1, p)
                    lo(u, p)
                    if p == 0:
                        norm_piece(u, 3)
                if u == 0:
                    u_norm(0)
                    for n in range(NQ):
                        u_low(n)
                        if n + 1 < NQ:
                            u_norm(n + 1)
                if q:
                    stats1(t)
                for c in cs[:5]:
                    chunk(c)
                lo(u, NQ)
                if q:
                    for j in range(3):
                        round_piece(t, j)
                if has_last(u):
                    x1_unit(u + 1, NQ - 1)
                    stats2(u + 1)
                elif u + 1 < NT:
                    column_correction(u // TB + 1, 0)
                for n in range(NQ):
                    if n == NQ - 1 and (u + 1) % TB:
                        for p in range(3):
                            norm_piece(u + 1, p)
                    y_unit(u, n)
                    if q and n < 2:
                        qT_piece(t, n)
                    if q and n == 0:
                        round_piece(t, 3)
                    if q and n == 2:
                        qT_piece(t, 2)
                        qT_piece(t, 3)
                    for c in cs[5 + n:6 + n]:
                        chunk(c)
                if q:
                    row_correction(t)

            constants()
            for b in range(NB):
                pair(b)
                for u in range(TB * b, TB * b + TB):
                    stage2_block(u)


_INS = ['x', 'ctx_4096', 'g_xattn', 'g_ffn', 'L0_xattn_x1_scale', 'L0_xattn_x1_zp', 'L0_xattn_x2_scale',
        'L0_xattn_x2_zp', 'L0_ffn_U', 'L0_ffn_S', 'L0_ffn_V']
_OUTS = [((2, 1024, 2048), 'float32')]


def kernel(**inputs):
    import numpy as _np
    import concourse.bacc as _bacc
    from concourse import mybir as _mybir
    from concourse.bass_utils import run_bass_kernel_spmd as _run

    nc = _bacc.Bacc("TRN2", target_bir_lowering=False, num_devices=1)
    arrays, args = {}, []
    for name in _INS:
        a = _np.ascontiguousarray(inputs[name])
        arrays[f"in_{name}_dram"] = a
        args.append(nc.dram_tensor(f"in_{name}_dram", a.shape, _mybir.dt.from_np(a.dtype), kind="ExternalInput").ap())
    for i, (shape, dtype) in enumerate(_OUTS):
        dt = _mybir.dt.from_np(_np.dtype(dtype))
        args.append(nc.dram_tensor(f"out_{i}_dram", shape, dt, kind="ExternalOutput").ap())
    gated_block_program(nc, *args)
    r = _run(nc, [arrays], core_ids=[0])
    return r.results[0]["out_0_dram"]
```

```python
import concourse.bass as bass
from concourse import mybir
from contextlib import ExitStack


def gated_block_program(nc, x, ctx_in, g_xattn, g_ffn, s1, z1, s2, z2, U, S, V, out):
    f32, bf16, f16, i32 = mybir.dt.float32, mybir.dt.bfloat16, mybir.dt.float16, mybir.dt.int32
    ALU, ACT, AX = mybir.AluOpType, mybir.ActivationFunctionType, mybir.AxisListType

    P = 128
    NB, SEQ, D = x.shape
    RANK = V.shape[1]
    KT = D // P
    RT = RANK // P
    W = 512
    NQ = D // W
    TB = SEQ // P
    NT = NB * TB
    CK = 2
    CQ = KT // CK
    CB = NQ * CQ
    NST = 4
    EPS = 1e-5
    MAGIC = 1.5 * 2.0 ** 23
    XS = 2.0 ** 9
    WS = 2.0 ** 14
    HS = 2.0 ** -15

    x_rows = x.rearrange("b s d -> (b s) d")
    out_rows = out.rearrange("b s d -> (b s) d")
    ctx_k = ctx_in.rearrange("b (k p) n -> b p k n", p=P)
    V_k = V.rearrange("(k p) r -> p k r", p=P)
    U_o = U.rearrange("(o p) r -> p o r", p=P)

    es = ExitStack()
    with es:
        def sb(name, shape, dt):
            return es.enter_context(nc.sbuf_tensor(name, shape, dt))

        def sem(name):
            return es.enter_context(nc.semaphore(name))

        q2 = sb("q2", [P, NQ, KT, W], bf16)
        v_hl = sb("v_hl", [P, KT, 2, W], f16)
        u_hl = sb("u_hl", [P, NQ, RT, 2, W], f16)
        ring = sb("ring", [P, 3, D], f32)
        qT = sb("qT", [P, 2, KT, P], bf16)
        xT_hi = sb("xT_hi", [P, KT, P], f16)
        xT_lo = sb("xT_lo", [P, KT, P], f16)
        piece = sb("piece", [P, 3, W], f32)
        qn = sb("qn", [P, 2, W], bf16)
        stage = sb("stage", [P, NST, CK, W], f32)
        hT_hi = sb("hT_hi", [P, RT, P], f16)
        hT_lo = sb("hT_lo", [P, RT, P], f16)
        corr = sb("corr", [P, D], f32)
        ident_f = sb("ident_f", [P, P], f32)
        ident_b = sb("ident_b", [P, P], bf16)
        ones_f = sb("ones_f", [P, P], f32)
        ones_b = sb("ones_b", [P, P], bf16)
        par = sb("par", [P, 6], f32)
        s_col = sb("s_col", [P, RT], f32)
        const = sb("const", [P, 24], f32)
        st1 = sb("st1", [P, NQ, 6], f32)
        st2 = sb("st2", [P, 2, NQ, 6], f32)
        ln1 = sb("ln1", [P, 8], f32)
        ln2 = sb("ln2", [P, 2, 8], f32)
        r1p = sb("r1p", [P, 2, NQ], f32)
        bvec = sb("bvec", [P, 2, 2], f32)
        ssq = sb("ssq", [P, 8 + 2 * NQ], f32)
        wsc = sb("wsc", [P, 4, 1 + NQ], f32)
        us_scale = sb("us_scale", [P, NQ, RT], f32)
        cy = sb("cy", [P, NQ], f32)

        def bank(name):
            return es.enter_context(nc.psum_tensor(name, [P, W], f32))

        acc = [bank("acc0"), bank("acc1")]
        hP = bank("hP")
        yP = [bank("y0"), bank("y1")]
        T = [bank("t0"), bank("t1"), bank("t2")]

        v_raw = u_hl[:, :, :, :, :].rearrange("p n r a w -> p (n r) (a w)").bitcast(f32)
        s_all = xT_hi[:, 0:2 * RT, :].rearrange("p k w -> p (k w)").bitcast(f32)
        junk_v = xT_lo[:, 0:8, :].rearrange("p k w -> p (k w)").bitcast(bf16)
        junk_u = qn[:, :, :].rearrange("p a w -> p (a w)")

        (C_R1, C_R2, _, _, C_MC1, C_MC2, _, C_F2, C_TG1, C_TG2, C_AF1, C_AF2, C_A, C_AFF,
         C_SMAX, C_SMIN, C_TV) = [const[:, i:i + 1] for i in range(17)]
        C_R, C_C, C_MC, C_F, C_TG, C_AF = [const[:, i:i + 2] for i in range(0, 12, 2)]
        P_S1, P_S2, P_Z1, P_Z2 = [par[:, i:i + 1] for i in range(4)]
        P_S, P_Z, P_G = par[:, 0:2], par[:, 2:4], par[:, 4:6]

        par_in = sem("par_in")
        x_in = sem("x_in")
        x0_in = [sem(f"x0_in{n}") for n in range(NQ)]
        s_in = sem("s_in")
        stage_in = [sem(f"stage_in{i}") for i in range(NST)]
        u_in = sem("u_in")
        v_in = [sem(f"v_in{i}") for i in range(4)]
        y_stored = sem("y_stored")
        setup_ready = sem("setup_ready")
        tanh_ready = sem("tanh_ready")
        const_step = sem("const_step")
        ctx_scaled = sem("ctx_scaled")
        ctx_round = sem("ctx_round")
        q2_ready = sem("q2_ready")
        colsum_done = sem("colsum_done")
        corr_ready = sem("corr_ready")
        ln1_step = sem("ln1_step")
        ln1_sqrt = sem("ln1_sqrt")
        ln1_agg = sem("ln1_agg")
        ln1_agg2 = sem("ln1_agg2")
        st2_ready = sem("st2_ready")
        ln2_step = sem("ln2_step")
        ln2_sqrt = sem("ln2_sqrt")
        q_relu = sem("q_relu")
        q_round = sem("q_round")
        q_ready = sem("q_ready")
        t_written = sem("t_written")
        t_read = sem("t_read")
        row_step = sem("row_step")
        xc_ready = sem("xc_ready")
        s1_done = sem("s1_done")
        x1_ready = sem("x1_ready")
        xs_ready = sem("xs_ready")
        t_hi = sem("t_hi")
        mm3_done = sem("mm3_done")
        h_evac = sem("h_evac")
        y_done = sem("y_done")
        y_ready = sem("y_ready")
        sq_done = sem("sq_done")
        norm_sum = sem("norm_sum")
        norm_step = sem("norm_step")
        norm_sqrt = sem("norm_sqrt")
        split_hi = sem("split_hi")
        split_lo = sem("split_lo")
        ut_done = sem("ut_done")

        def base(u):
            return 2 * NQ + (2 * NQ + 1) * u - (NQ if u == NT - 1 else 0)

        def x_piece(u, p):
            return base(u) + p

        def h_piece(u):
            return base(u) + NQ

        def q_piece(t, j):
            return NQ * t + j if t < 2 else base(t - 2) + NQ + 1 + j

        def s1_unit(t, n):
            b, m = t // TB, t % TB
            if m < 2:
                return NQ * TB * b + {(NQ - 1, 0): 2 * NQ - 3, (NQ - 2, 1): 2 * NQ - 2}.get((n, m), 2 * n + m)
            return NQ * (TB * b + m) + n

        def stage_count(c):
            extra = (2 if c % NST < KT // NQ // CK else 1) if c >= CB else 0
            return 16 * (c // NST + 1 + extra)

        VP = KT // 2
        V_START = 3

        def v_pairs(i):
            split = lambda j: max(0, j * VP // (2 * CQ - V_START))
            return [(k - NQ // 2) % VP for k in range(split(i - V_START), split(i - V_START + 1))]

        UC = KT // NQ // CK

        def u_raw(n, k):
            return v_raw[:, 3 * NQ + k, :] if n == 2 else stage[:, n % 3 * UC + k // CK, k % CK, :]

        N_CONST = 9
        N_FIRST = 1
        NORM_STEPS = 7
        GROUPS = ((0, 1), (1, NQ), (NQ, NQ + 1))

        AHEAD = {TB - 2: (1, 1, 1, 3, 1, 0, 1, 0, 0), TB - 1: (0, 0, 4, 1, 1, 2, 1, 0, 4)}
        N_AHEAD = sum(AHEAD[TB - 2]) + sum(AHEAD[TB - 1])
        ACT_AHEAD = 2

        def boundary_chunks(u):
            b, m = u // TB + 1, u % TB
            sizes = AHEAD.get(m, (0,) * 9) if b < NB else (0,) * 9
            c = CB * b + (sum(AHEAD[TB - 2]) if m == TB - 1 else 0)
            return [range(c + sum(sizes[:i]), c + sum(sizes[:i + 1])) for i in range(len(sizes))]

        has_s1 = lambda u: u % TB not in (0, TB - 1)
        has_last = lambda u: u % TB != TB - 1

        def unit_bank(t, n):
            m = t % TB
            return (yP, acc)[n % 2][m] if m < 2 else acc[s1_unit(t, n) % 2]

        def colsum_bank(b, n):
            return T[1] if n == 2 else acc[0] if b > 0 and n == 0 else hP

        u_bank = lambda q: (yP[0], acc[1], T[1], T[2])[q % 4]
        xq = lambda t, n: ring[:, t % 3, n * W:(n + 1) * W]
        tiles_of = lambda b: (TB * b, TB * b + 1)

        block = es.enter_context(nc.Block())

        @block.gpsimd
        def _(pool):
            nc.gpsimd.memset(ident_f[:, :], 0.0)
            nc.gpsimd.memset(ident_b[:, :], 0.0)
            nc.gpsimd.memset(ones_f[:, :], 1.0)
            nc.gpsimd.memset(ones_b[:, :], 1.0).then_inc(setup_ready, 1)
            pool.wait_ge(setup_ready, 1)
            for m in (ident_f, ident_b):
                nc.gpsimd.affine_select(out=m[:, :], in_=m[:, :], compare_op=ALU.not_equal, fill=1.0,
                                        base=0, pattern=[[-1, P]], channel_multiplier=1)\
                    .then_inc(setup_ready, 1)

        @block.sync
        def _(sp):
            def load_x(t):
                if t >= 3:
                    sp.wait_ge(y_stored, 32 * (t - 2))
                if t >= 2:
                    sp.wait_ge(x_in, 16 * (t - 1))
                sp.dma_start(ring[:, t % 3, :], x_rows[t * P:(t + 1) * P, :]).then_inc(x_in, 16)

            def load_chunks(b, n, first=0, end=CQ):
                for i in range(first, end):
                    c = CB * b + CQ * n + i
                    if NST <= c < CB or c >= CB + NST:
                        sp.wait_ge(q2_ready, c - NST + 1)
                    elif c >= CB:
                        sp.wait_ge(ut_done, NQ * RT)
                    sp.dma_start(stage[:, c % NST, :, :],
                                 ctx_k[b, :, CK * i:CK * i + CK, n * W:(n + 1) * W])\
                        .then_inc(stage_in[c % NST], 16)

            for i, a in enumerate((s1, s2, z1, z2, g_xattn, g_ffn)):
                with nc.allow_non_contiguous_dma(reason="one scalar to all partitions"):
                    sp.dma_start(par[:, i:i + 1], a.rearrange("(o a) -> o a", o=1).to_broadcast([P, 1]))\
                        .then_inc(par_in, 16)
            with nc.allow_non_contiguous_dma(reason="512 scales"):
                sp.dma_start(s_col[:, :], S.rearrange("(r p) -> p r", p=P)).then_inc(par_in, 16)
            load_chunks(0, 0, 0, CQ - 2)
            load_x(1)
            load_chunks(0, 0, CQ - 2, CQ)
            for i in range(CQ):
                load_chunks(0, 1, i, i + 1)
                sp.dma_start(v_raw[:, 2 * i:2 * i + 2, :], V_k[:, 2 * i:2 * i + 2, :]).then_inc(v_in[i // 2], 16)
            sp.dma_start(s_all, S.rearrange("(o a) -> o a", o=1).to_broadcast([P, RANK])).then_inc(s_in, 16)
            load_chunks(0, 2)
            load_chunks(0, 3, 0, 3)
            sp.wait_ge(split_lo, NQ // 2)
            sp.dma_start(v_raw[:, 3 * NQ:KT, :], U_o[:, 2 * NQ:3 * NQ, :]).then_inc(u_in, 16)
            load_chunks(0, 3, 3, CQ)
            for i in range(NST):
                sp.wait_ge(q2_ready, CB - NST + i + 1)
                sp.dma_start(stage[:, i, :, :], U_o[:, CK * i:CK * i + CK, :]).then_inc(stage_in[i], 16)
            load_x(2)
            sp.wait_ge(ut_done, RT)
            for i in range(UC):
                sp.dma_start(stage[:, i, :, :], U_o[:, 3 * NQ + CK * i:3 * NQ + CK * i + CK, :])\
                    .then_inc(stage_in[i], 16)
            for u in range(NT - 3):
                if u % TB == TB - 3:
                    load_chunks(u // TB + 1, 0, 0, NST)
                if u % TB == TB - 2:
                    load_chunks(u // TB + 1, 0, NST, CQ)
                    load_chunks(u // TB + 1, 1, 0, NST)
                if u % TB == TB - 1:
                    load_chunks(u // TB + 1, 1, NST, CQ)
                    for n in range(2, NQ):
                        load_chunks(u // TB + 1, n)
                load_x(u + 3)

        @block.tensor
        def _(pe):
            def q_transpose(t, j):
                i = q_piece(t, j)
                pe.wait_ge(q_ready, NQ * t + j + 1)
                if i >= 3:
                    pe.wait_ge(t_read, i - 2)
                dst = T[i % 3][:, 0:W // 2].bitcast(bf16)
                for k in range(4):
                    mm = nc.tensor.transpose(dst[:, k * P:(k + 1) * P], qn[:, j % 2, k * P:(k + 1) * P], ident_b[:, :])
                mm.then_inc(t_written, 1)

            def f_transpose(i):
                pe.wait_ge(t_read, i - 2)
                for k in range(4):
                    mm = nc.tensor.transpose(T[i % 3][:, k * P:(k + 1) * P], piece[:, i % 3, k * P:(k + 1) * P],
                                             ident_f[:, :])
                mm.then_inc(t_written, 1)

            def x_transpose(u, p):
                pe.wait_ge(xs_ready, NQ * u + p + 1)
                f_transpose(x_piece(u, p))

            def colsum(b, n, k0=0, k1=KT):
                if k0 == 0 and b > 0 and n == 0:
                    pe.wait_ge(x1_ready, NQ * TB * b)
                if k0 == 0 and b > 0 and n == 1:
                    pe.wait_ge(h_evac, TB * b)
                if k0 == 0 and n == 2:
                    pe.wait_ge(t_read, q_piece(TB * b + 1, NQ - 1) + 1)
                if k0 == 0 and n in (1, 3):
                    pe.wait_ge(corr_ready, NQ * b + (n + 1) // 2)
                for k in range(k0, k1):
                    if k % CK == 0:
                        pe.wait_ge(q2_ready, CB * b + CQ * n + k // CK + 1)
                    mm = nc.tensor.matmul(colsum_bank(b, n)[:, :], ones_b[:, :], q2[:, n, k, :],
                                          start=(k == 0), stop=(k == KT - 1))
                if k1 == KT:
                    mm.then_inc(colsum_done, 1)

            def s1_part(t, n, k0, k1):
                i, b, m = s1_unit(t, n), t // TB, t % TB
                if k0 == 0:
                    pe.wait_ge(t_read, q_piece(t, NQ - 1) + 1)
                    if m >= 2:
                        pe.wait_ge(x1_ready, i - 1)
                    elif n >= 2:
                        pe.wait_ge(x1_ready, s1_unit(t, n - 2) + 1)
                    elif b > 0 and n == 0:
                        pe.wait_ge(y_ready, NQ * TB * b - 1 + m)
                    elif b > 0:
                        pe.wait_ge(x1_ready, NQ * TB * b)
                        pe.wait_ge(corr_ready, NQ * b + 1)
                    if i in (7, 8):
                        pe.wait_ge(split_lo, VP + RT * NQ - 2)
                for k in range(k0, k1):
                    mm = nc.tensor.matmul(unit_bank(t, n)[:, :], qT[:, t % 2, k, :], q2[:, n, k, :],
                                          start=(k == 0), stop=(k == KT - 1))
                if k1 == KT:
                    mm.then_inc(s1_done, 1)

            def mm3(u, k0=0, k1=KT):
                if k0 == 0:
                    pe.wait_ge(corr_ready, NQ * (u // TB + 1))
                    if u == 0:
                        pe.wait_ge(split_lo, VP)
                    else:
                        pe.wait_ge(h_evac, u)
                for k in range(k0, k1):
                    if k % 4 == 0:
                        pe.wait_ge(t_read, x_piece(u, k // 4) + 1)
                    nc.tensor.matmul(hP[:, :], xT_hi[:, k, :], v_hl[:, k, 0, :], start=(k == 0), stop=False)
                    nc.tensor.matmul(hP[:, :], xT_hi[:, k, :], v_hl[:, k, 1, :], start=False, stop=False)
                    mm = nc.tensor.matmul(hP[:, :], xT_lo[:, k, :], v_hl[:, k, 0, :], start=False, stop=(k == KT - 1))
                if k1 == KT:
                    mm.then_inc(mm3_done, 1)

            def mm4(u, n):
                i = NQ * u + n
                if n == 0:
                    pe.wait_ge(t_read, h_piece(u) + 1)
                if u % TB == 0 and n < 2:
                    pe.wait_ge(x1_ready, s1_unit(u + 1, 2) + 1)
                if u == 0:
                    pe.wait_ge(split_lo, VP + RT * NQ if n < 2 else VP + RT * (n + 1))
                if i >= 2:
                    pe.wait_ge(y_ready, i - 1)
                for r in range(RT):
                    nc.tensor.matmul(yP[i % 2][:, :], hT_hi[:, r, :], u_hl[:, n, r, 0, :], start=(r == 0), stop=False)
                    nc.tensor.matmul(yP[i % 2][:, :], hT_hi[:, r, :], u_hl[:, n, r, 1, :], start=False, stop=False)
                    mm = nc.tensor.matmul(yP[i % 2][:, :], hT_lo[:, r, :], u_hl[:, n, r, 0, :],
                                          start=False, stop=(r == RT - 1))
                mm.then_inc(y_done, 1)

            def pair(b):
                t0, t1 = tiles_of(b)
                if b == 0:
                    pe.wait_ge(setup_ready, 3)
                    for j in range(NQ):
                        q_transpose(t0, j)
                for n in range(NQ):
                    step = CK if n == NQ - 1 or b == 0 and n != 1 else KT
                    for k in range(0, KT, step):
                        if b == 0 or n > 0:
                            colsum(b, n, k, k + step)
                        s1_part(t0, n, k, k + step)
                    if b == 0 and n == 0:
                        for j in range(NQ):
                            q_transpose(t1, j)
                    if b == 0 and n == 1:
                        pe.wait_ge(sq_done, 8)
                        nc.tensor.matmul(T[2][:, 0:8], ones_f[:, :], ssq[:, 0:8], start=True, stop=True)\
                            .then_inc(norm_sum, 1)
                    if n < NQ - 2:
                        s1_part(t1, n, 0, KT)
                s1_part(t1, NQ - 2, 0, KT)

            def u_norm(g):
                c = slice(8 + 2 * (GROUPS[g][0] - 1), 8 + 2 * (GROUPS[g][1] - 1))
                pe.wait_ge(sq_done, c.stop)
                if g == 1:
                    pe.wait_ge(x1_ready, s1_unit(0, NQ - 1) + 1)
                else:
                    pe.wait_ge(norm_step, NORM_STEPS + 1)
                nc.tensor.matmul(acc[0][:, c], ones_f[:, :], ssq[:, c], start=True, stop=True).then_inc(norm_sum, 1)

            def u_transpose(n):
                if n == 0:
                    pe.wait_ge(t_read, x_piece(0, NQ - 1) + 1)
                for r in range(RT):
                    q = RT * n + r
                    if q >= 4:
                        pe.wait_ge(split_lo, VP + q - 3)
                    for k in range(4):
                        mm = nc.tensor.transpose(u_bank(q)[:, k * P:(k + 1) * P],
                                                 u_raw(n, k)[:, r * P:(r + 1) * P], ident_f[:, :])
                    mm.then_inc(ut_done, 1)

            def stage2_block(u):
                t = u + 1
                if has_s1(u):
                    for n in range(NQ - 1):
                        s1_part(t, n, 0, KT)
                        x_transpose(u, n)
                    x_transpose(u, NQ - 1)
                else:
                    if u == 0:
                        pe.wait_ge(norm_step, 1)
                    for p in range(NQ):
                        x_transpose(u, p)
                if u == 0:
                    u_norm(1)
                    for n in range(NQ):
                        u_transpose(n)
                        if n == 2:
                            u_norm(2)
                        mm3(u, 4 * n, 4 * n + 4)
                else:
                    mm3(u)
                fill = None
                if has_last(u):
                    fill = lambda k0, k1: s1_part(t, NQ - 1, k0, k1)
                elif u + 1 < NT:
                    fill = lambda k0, k1: colsum(u // TB + 1, 0, k0, k1)
                if fill:
                    fill(0, KT // 2)
                pe.wait_ge(h_evac, u + 1)
                f_transpose(h_piece(u))
                if fill:
                    fill(KT // 2, KT)
                q = u + 2 < NT
                for n in range(NQ):
                    mm4(u, n)
                    if q and n < 2:
                        q_transpose(u + 2, n)
                    if q and n == 2:
                        q_transpose(u + 2, 2)
                        q_transpose(u + 2, 3)

            for b in range(NB):
                pair(b)
                for u in range(TB * b, TB * b + TB):
                    stage2_block(u)

        @block.scalar
        def _(act):
            def chunks(cs):
                for c in cs:
                    act.wait_ge(stage_in[c % NST], stage_count(c))
                    a = stage[:, c % NST, :, :]
                    nc.scalar.activation(a, a, ACT.Relu, bias=P_Z2, scale=C_R2).then_inc(ctx_scaled, 1)

            def sqrt1(t):
                act.wait_ge(ln1_step, 6 * t + 2)
                nc.scalar.activation(ln1[:, 3:4], ln1[:, 2:3], ACT.Sqrt).then_inc(ln1_sqrt, 1)

            def sqrt2(u):
                act.wait_ge(ln2_step, 6 * u + 2)
                nc.scalar.activation(ln2[:, u % 2, 3:4], ln2[:, u % 2, 2:3], ACT.Sqrt).then_inc(ln2_sqrt, 1)

            def relu(t, j):
                i = q_piece(t, j)
                act.wait_ge(ln1_step, 6 * t + 6)
                if i >= 3:
                    act.wait_ge(t_written, i - 2)
                nc.scalar.activation(piece[:, i % 3, :], xq(t, j), ACT.Relu, bias=ln1[:, 6:7], scale=ln1[:, 5:6])\
                    .then_inc(q_relu, 1)

            def centre(t, j):
                i = q_piece(t, j)
                act.wait_ge(q_round, NQ * t + j + 1)
                if NQ * t + j >= 2:
                    ip = q_piece(t, j - 2) if j >= 2 else q_piece(t - 1, j + 2)
                    act.wait_ge(t_written, ip + 1)
                if t >= 2:
                    act.wait_ge(row_step, 2 * (t - 1))
                if t == 2 and j < 2:
                    act.wait_ge(sq_done, 8 + 2 * NQ)
                nc.scalar.activation(qn[:, j % 2, :], piece[:, i % 3, :], ACT.Identity, bias=C_MC1,
                                     accum_out=r1p[:, t % 2, j:j + 1]).then_inc(q_ready, 1)

            def hi(i, dst):
                act.wait_ge(t_written, i + 1)
                nc.scalar.activation(dst, T[i % 3][:, :], ACT.Copy).then_inc(t_hi, 1)

            def h_out(u):
                i = h_piece(u)
                act.wait_ge(mm3_done, u + 1)
                act.wait_ge(t_written, i - 2)
                nc.scalar.activation(piece[:, i % 3, :], hP[:, :], ACT.Copy, scale=HS).then_inc(h_evac, 1)

            def column_correction(b, n):
                act.wait_ge(colsum_done, NQ * b + n + 1)
                if b > 0:
                    act.wait_ge(xc_ready, NQ * TB * b)
                nc.scalar.activation(corr[:, n * W:(n + 1) * W], colsum_bank(b, n)[:, :], ACT.Identity,
                                     bias=C_AFF, scale=C_AF1).then_inc(corr_ready, 1)

            squares = [0]

            def square(i, src, junk):
                if squares[0]:
                    act.wait_ge(sq_done, squares[0])
                squares[0] += 1
                nc.scalar.activation(junk, src.rearrange("p k w -> p (k w)"), ACT.Square, accum_out=ssq[:, i:i + 1])\
                    .then_inc(sq_done, 1)

            def norm_root(g):
                w = slice(*GROUPS[g])
                act.wait_ge(norm_step, NORM_STEPS * g + 1)
                nc.scalar.activation(wsc[:, 1, w], wsc[:, 0, w], ACT.Sqrt).then_inc(norm_sqrt, 1)

            def v_high(j):
                act.wait_ge(norm_step, NORM_STEPS)
                k = slice(2 * j, 2 * j + 2)
                nc.scalar.activation(v_hl[:, k, 0, :], v_raw[:, k, :], ACT.Copy, scale=wsc[:, 3, 0:1])\
                    .then_inc(split_hi, 1)

            def u_squares(n):
                for i in range(UC):
                    if n == 2:
                        act.wait_ge(u_in, 16)
                        src = v_raw[:, 3 * NQ + CK * i:3 * NQ + CK * i + CK, :]
                    else:
                        s = n % 3 * UC + i
                        act.wait_ge(stage_in[s], 16 * (CB // NST + 1 + n // 3))
                        src = stage[:, s, :, :]
                    square(8 + UC * n + i, src, junk_u)

            def v_squares(i):
                act.wait_ge(v_in[i // 2], 32)
                square(i, v_raw[:, 2 * i:2 * i + 2, :], junk_v)

            def u_high(n, rs):
                act.wait_ge(norm_step, NORM_STEPS * (2 + n // 3))
                for r in rs:
                    q = RT * n + r
                    act.wait_ge(split_lo, VP)
                    act.wait_ge(ut_done, q + 1)
                    nc.scalar.activation(u_hl[:, n, r, 0, :], u_bank(q)[:, :], ACT.Copy, scale=us_scale[:, n, r:r + 1])\
                        .then_inc(split_hi, 1)

            def pair(b):
                t0, t1 = tiles_of(b)
                if b == 0:
                    for n in range(NQ):
                        act.dma_start(xq(0, n), x_rows[0:P, n * W:(n + 1) * W]).then_inc(x0_in[n], 16)
                    act.wait_ge(par_in, 16 * 7)
                    nc.scalar.activation(C_TG, P_G, ACT.Tanh).then_inc(tanh_ready, 1)
                    act.wait_ge(const_step, N_FIRST)
                    quantise(t0, range(0, CQ))
                    quantise(t1, range(CQ, 2 * CQ))
                    v_squares(2)
                    v_squares(3)
                    for i in range(2):
                        chunks([2 * CQ + i])
                        v_squares(2 * i + 4)
                        v_squares(2 * i + 5)
                    column_correction(0, 1)
                    chunks([2 * CQ + 2])
                    norm_root(0)
                    for i in range(V_START, 2 * CQ):
                        chunks([2 * CQ + i])
                        for j in v_pairs(i):
                            v_high(j)
                        if i == CQ + 1:
                            column_correction(0, 2)
                            act.wait_ge(t_written, q_piece(t1, NQ - 1) + 1)
                            u_squares(2)
                    u_squares(0)
                    column_correction(0, 3)
                    u_squares(1)
                else:
                    c = CB * b + N_AHEAD + ACT_AHEAD
                    chunks(range(c, c + 5))
                    column_correction(b, 1)
                    chunks(range(c + 5, CB * b + CB))
                    column_correction(b, 2)
                    column_correction(b, 3)
                sqrt2(t0)

            def quantise(t, cs):
                if t == 0:
                    sqrt1(t)
                chunks(cs[0:2])
                if t > 0:
                    sqrt1(t)
                chunks(cs[2:3])
                for j in range(3):
                    relu(t, j)
                chunks(cs[3:4])
                if t == 0:
                    act.wait_ge(const_step, N_CONST)
                else:
                    v_squares(0)
                    column_correction(0, 0)
                centre(t, 0)
                centre(t, 1)
                chunks(cs[4:5])
                relu(t, 3)
                centre(t, 2)
                chunks(cs[5:6])
                centre(t, 3)
                if t > 0:
                    v_squares(1)
                chunks(cs[6:8])

            def store(u, n0, n1):
                act.wait_ge(y_ready, NQ * u + n1)
                c = slice(n0 * W, n1 * W)
                act.dma_start(out_rows[u * P:(u + 1) * P, c], ring[:, u % 3, c]).then_inc(y_stored, 16)

            def stage2_block(u):
                q, t = u + 2 < NT, u + 2
                cs = boundary_chunks(u)
                for p in range(NQ):
                    hi(x_piece(u, p), xT_hi[:, 4 * p:4 * p + 4, :].rearrange("p k w -> p (k w)"))
                    if p == 2 and u % TB == TB - 1:
                        store(u - 1, 2, NQ)
                    if p > 0:
                        chunks(cs[p - 1])
                if u == 0:
                    norm_root(1)
                    for n in range(NQ):
                        u_high(n, (0, 1))
                        if n == 1:
                            sqrt1(2)
                        u_high(n, (2, 3))
                        if n == 1:
                            u_squares(3)
                        if n == 2:
                            norm_root(2)
                if q and u > 0:
                    sqrt1(t)
                chunks(cs[3])
                h_out(u)
                hi(h_piece(u), hT_hi[:, :, :].rearrange("p k w -> p (k w)"))
                chunks(cs[4])
                if q:
                    for j in range(3):
                        relu(t, j)
                    centre(t, 0)
                    centre(t, 1)
                chunks(cs[5])
                if q:
                    relu(t, 3)
                if has_last(u):
                    sqrt2(u + 1)
                if q:
                    centre(t, 2)
                    centre(t, 3)
                if u % TB == TB - 1 and u + 1 < NT:
                    column_correction(u // TB + 1, 0)
                for n in range(1, NQ):
                    chunks(cs[5 + n])
                store(u, 0, 2)
                if u % TB == TB - 1 and u + 1 < NT:
                    chunks(range(cs[-1].stop, cs[-1].stop + ACT_AHEAD))
                if u == NT - 1:
                    store(u, 2, 3)
                    store(u, 3, NQ)
                elif u % TB != TB - 2:
                    store(u, 2, NQ)

            for b in range(NB):
                pair(b)
                for u in range(TB * b, TB * b + TB):
                    stage2_block(u)
            act.wait_ge(y_stored, 32 * NT + 16)

        const_steps = [0]

        @block.vector
        def _(dve):
            ts, stt, tt = nc.vector.tensor_scalar, nc.vector.scalar_tensor_tensor, nc.vector.tensor_tensor

            def step(ins):
                const_steps[0] += 1
                ins.then_inc(const_step, 1)
                dve.wait_ge(const_step, const_steps[0])

            def first_constants():
                dve.wait_ge(par_in, 16 * 7)
                step(nc.vector.reciprocal(C_R, P_S))

            def constants():
                step(ts(C_C, P_Z, 0.0, 255.0, ALU.max, ALU.min))
                step(ts(C_MC, C_C, MAGIC, None, ALU.add))
                step(ts(C_C, C_MC, MAGIC, None, ALU.subtract))
                step(tt(C_F, P_Z, C_C, ALU.subtract))
                step(ts(C_MC, C_MC, -1.0, None, ALU.mult))
                dve.wait_ge(tanh_ready, 1)
                step(stt(C_A, C_TG1, P_S1, P_S2, ALU.mult, ALU.mult))
                step(ts(C_AF, C_F, C_A, -1.0, ALU.mult, ALU.mult))
                step(stt(C_AFF, C_AF1, -float(D), C_F2, ALU.mult, ALU.mult))

            def largest_s():
                dve.wait_ge(s_in, 16)
                step(nc.vector.tensor_reduce(C_SMAX, s_all, AX.X, ALU.max))
                step(nc.vector.tensor_reduce(C_SMIN, s_all, AX.X, ALU.min))
                step(stt(C_SMAX, C_SMIN, -1.0, C_SMAX, ALU.mult, ALU.max))

            def stats1_sums(t):
                s = 6 * t
                if t >= 1:
                    dve.wait_ge(x_in, 16 * t)
                    dve.wait_ge(q_relu, NQ * t)
                for n in range(NQ):
                    if t == 0:
                        dve.wait_ge(x0_in[n], 16)
                    ins = nc.vector.bn_stats(st1[:, n, :], xq(t, n))
                ins.then_inc(ln1_step, 1)
                dve.wait_ge(ln1_step, s + 1)
                nc.vector.bn_aggr(ln1[:, 0:2], st1[:, :, :]).then_inc(ln1_agg, 1)
                dve.wait_ge(ln1_agg, t + 1)
                ts(ln1[:, 2:3], ln1[:, 1:2], EPS, None, ALU.add).then_inc(ln1_step, 1)

            def stats1(t):
                s = 6 * t
                if t > 0:
                    stats1_sums(t)
                else:
                    constants()
                dve.wait_ge(ln1_sqrt, t + 1)
                nc.vector.reciprocal(ln1[:, 4:5], ln1[:, 3:4]).then_inc(ln1_step, 1)
                dve.wait_ge(ln1_step, s + 3)
                stt(ln1[:, 7:8], ln1[:, 4:5], ln1[:, 2:3], ln1[:, 4:5], ALU.mult, ALU.mult).then_inc(ln1_step, 1)
                dve.wait_ge(ln1_step, s + 4)
                ts(ln1[:, 7:8], ln1[:, 7:8], -0.5, 1.5, ALU.mult, ALU.add).then_inc(ln1_agg2, 1)
                dve.wait_ge(ln1_agg2, 2 * t + 1)
                stt(ln1[:, 5:6], ln1[:, 4:5], C_R1, ln1[:, 7:8], ALU.mult, ALU.mult).then_inc(ln1_step, 1)
                dve.wait_ge(ln1_step, s + 5)
                stt(ln1[:, 7:8], ln1[:, 0:1], -1.0, ln1[:, 5:6], ALU.mult, ALU.mult).then_inc(ln1_agg2, 1)
                dve.wait_ge(ln1_agg2, 2 * t + 2)
                tt(ln1[:, 6:7], ln1[:, 7:8], P_Z1, ALU.add).then_inc(ln1_step, 1)

            def stats2(u):
                s, v = 6 * u, ln2[:, u % 2, :]
                dve.wait_ge(st2_ready, s1_unit(u, NQ - 1) + 1)
                nc.vector.bn_aggr(v[:, 0:2], st2[:, u % 2, :, :]).then_inc(ln2_step, 1)
                dve.wait_ge(ln2_step, s + 1)
                ts(v[:, 2:3], v[:, 1:2], EPS, None, ALU.add).then_inc(ln2_step, 1)
                dve.wait_ge(ln2_sqrt, u + 1)
                nc.vector.reciprocal(v[:, 4:5], v[:, 3:4]).then_inc(ln2_step, 1)
                dve.wait_ge(ln2_step, s + 3)
                stt(v[:, 7:8], v[:, 4:5], v[:, 2:3], v[:, 4:5], ALU.mult, ALU.mult).then_inc(ln2_step, 1)
                dve.wait_ge(ln2_step, s + 4)
                ts(v[:, 6:7], v[:, 7:8], -0.5, 1.5, ALU.mult, ALU.add).then_inc(ln2_step, 1)
                dve.wait_ge(ln2_step, s + 5)
                stt(v[:, 5:6], v[:, 4:5], XS, v[:, 6:7], ALU.mult, ALU.mult).then_inc(ln2_step, 1)

            def round_chunk(c):
                a = stage[:, c % NST, :, :]
                dve.wait_ge(ctx_scaled, c + 1)
                ts(a, a, 255.0, MAGIC, ALU.min, ALU.add).then_inc(ctx_round, 1)

            def store_chunk(c):
                b, n, i = c // CB, c % CB // CQ, c % CQ
                a = stage[:, c % NST, :, :]
                dve.wait_ge(ctx_round, c + 1)
                if b > 0 and i == 0:
                    dve.wait_ge(s1_done, s1_unit(TB * b - 1, n) + 1)
                ts(q2[:, n, CK * i:CK * i + CK, :], a, C_MC2, None, ALU.add).then_inc(q2_ready, 1)

            def row_correction(t):
                dve.wait_ge(q_ready, NQ * (t + 1))
                nc.vector.tensor_reduce(bvec[:, t % 2, 0:1], r1p[:, t % 2, :], AX.X, ALU.add).then_inc(row_step, 1)
                dve.wait_ge(row_step, 2 * t + 1)
                tt(bvec[:, t % 2, 1:2], bvec[:, t % 2, 0:1], C_AF2, ALU.mult).then_inc(row_step, 1)

            def x1_unit(t, n):
                i = s1_unit(t, n)
                dve.wait_ge(row_step, 2 * t + 2)
                dve.wait_ge(q_relu, NQ * (t + 1))
                dve.wait_ge(corr_ready, NQ * (t // TB) + n + 1)
                stt(xq(t, n), xq(t, n), bvec[:, t % 2, 1:2], corr[:, n * W:(n + 1) * W], ALU.add, ALU.add)\
                    .then_inc(xc_ready, 1)
                dve.wait_ge(xc_ready, i + 1)
                dve.wait_ge(s1_done, i + 1)
                stt(xq(t, n), unit_bank(t, n)[:, :], C_A, xq(t, n), ALU.mult, ALU.add).then_inc(x1_ready, 1)
                dve.wait_ge(x1_ready, i + 1)
                nc.vector.bn_stats(st2[:, t % 2, n, :], xq(t, n)).then_inc(st2_ready, 1)

            def norm_piece(u, p):
                i = x_piece(u, p)
                if p == 0:
                    dve.wait_ge(ln2_step, 6 * u + 6)
                dve.wait_ge(t_written, i - 2)
                ts(piece[:, i % 3, :], xq(u, p), ln2[:, u % 2, 0:1], ln2[:, u % 2, 5:6], ALU.subtract, ALU.mult)\
                    .then_inc(xs_ready, 1)

            def lo(u, p):
                if p < NQ:
                    i, k = x_piece(u, p), slice(4 * p, 4 * p + 4)
                    h, l = xT_hi[:, k, :], xT_lo[:, k, :]
                else:
                    i, h, l = h_piece(u), hT_hi[:, :, :], hT_lo[:, :, :]
                flat = lambda a: a.rearrange("p k w -> p (k w)")
                dve.wait_ge(t_hi, 5 * u + p + 1)
                tt(flat(l), T[i % 3][:, :], flat(h), ALU.subtract).then_inc(t_read, 1)

            def chunks(cs):
                for c in cs:
                    round_chunk(c)
                    if c > cs[0]:
                        store_chunk(c - 1)
                if len(cs):
                    store_chunk(cs[-1])

            def round_piece(t, j):
                i = q_piece(t, j)
                dve.wait_ge(q_relu, NQ * t + j + 1)
                ts(piece[:, i % 3, :], piece[:, i % 3, :], 255.0, MAGIC, ALU.min, ALU.add).then_inc(q_round, 1)

            def qT_piece(t, j):
                i = q_piece(t, j)
                dve.wait_ge(t_written, i + 1)
                nc.vector.tensor_copy(qT[:, t % 2, 4 * j:4 * j + 4, :].rearrange("p k w -> p (k w)"),
                                      T[i % 3][:, 0:W // 2].bitcast(bf16)).then_inc(t_read, 1)

            def y_unit(u, n):
                i = NQ * u + n
                dve.wait_ge(y_done, i + 1)
                stt(xq(u, n), yP[i % 2][:, :], cy[:, n:n + 1], xq(u, n), ALU.mult, ALU.add).then_inc(y_ready, 1)

            def quantise(t, cs):
                stats1(t)
                chunks(cs[0:3])
                for j in range(3):
                    round_piece(t, j)
                chunks(cs[3:4])
                qT_piece(t, 0)
                round_chunk(cs[4])
                round_piece(t, 3)
                store_chunk(cs[4])
                qT_piece(t, 1)
                round_chunk(cs[5])
                qT_piece(t, 2)
                store_chunk(cs[5])
                qT_piece(t, 3)
                row_correction(t)
                chunks(cs[6:8])

            def pair(b):
                t0, t1 = tiles_of(b)
                if b == 0:
                    quantise(t0, range(0, CQ))
                    quantise(t1, range(CQ, 2 * CQ))
                left, c = ((3, 2), (2, 2), (2, 0), (0, 0)), CB * b + N_AHEAD
                for n in range(NQ):
                    if b > 0:
                        chunks(range(c, c + left[n][0]))
                        c += left[n][0]
                    for i in range(CQ if b == 0 else 0):
                        if b == 0 and n == 0 and i == 0:
                            largest_s()
                        if n == 1 and i == V_START:
                            v_norm()
                        if 0 < n < NQ - 1:
                            round_chunk(CQ * (n + 1) + i)
                            for j in v_pairs(CQ * (n - 1) + i):
                                v_low(j)
                            store_chunk(CQ * (n + 1) + i)
                    x1_unit(t0, n)
                    if n < NQ - 2:
                        x1_unit(t1, n)
                    if b > 0:
                        chunks(range(c, c + left[n][1]))
                        c += left[n][1]
                stats2(t0)

            def norm(g, sums, factor):
                s, w = NORM_STEPS * g, slice(*GROUPS[g])
                total, root, power, scale = [wsc[:, i, w] for i in range(4)]
                dve.wait_ge(norm_sum, g + 1)
                nc.vector.tensor_reduce(total, sums, AX.X, ALU.add).then_inc(norm_step, 1)
                dve.wait_ge(norm_sqrt, g + 1)
                ts(root, root, factor, 1e-30, ALU.mult, ALU.max).then_inc(norm_step, 1)
                dve.wait_ge(norm_step, s + 2)
                ts(power.bitcast(i32), root.bitcast(i32), 0x7F800000, None, ALU.bitwise_and)\
                    .then_inc(norm_step, 1)
                dve.wait_ge(norm_step, s + 3)
                nc.vector.reciprocal(scale, power).then_inc(norm_step, 1)
                dve.wait_ge(norm_step, s + 4)
                ts(scale, scale, WS, None, ALU.mult).then_inc(norm_step, 1)
                dve.wait_ge(norm_step, s + 5)

            def v_norm():
                norm(0, T[2][:, 0:8], 1.0)
                ts(C_TV, wsc[:, 2, 0:1], 1.0 / (XS * HS * WS * WS), None, ALU.mult).then_inc(norm_step, 1)
                dve.wait_ge(norm_step, NORM_STEPS - 1)
                tt(C_TV, C_TV, C_TG2, ALU.mult).then_inc(norm_step, 1)
                dve.wait_ge(norm_step, NORM_STEPS)

            def v_low(j):
                k = slice(2 * j, 2 * j + 2)
                dve.wait_ge(split_hi, (j + NQ // 2) % VP + 1)
                stt(v_hl[:, k, 1, :], v_raw[:, k, :], wsc[:, 3, 0:1], v_hl[:, k, 0, :], ALU.mult, ALU.subtract)\
                    .then_inc(split_lo, 1)

            def u_norm(g):
                w0, w1 = GROUPS[g]
                sums = acc[0][:, 8 + 2 * (w0 - 1):8 + 2 * (w1 - 1)].rearrange("p (n a) -> p n a", a=2)
                norm(g, sums, C_SMAX)
                ts(cy[:, w0 - 1:w1 - 1], wsc[:, 2, w0:w1], C_TV, None, ALU.mult).then_inc(norm_step, 1)
                for w in range(w0, w1):
                    ins = ts(us_scale[:, w - 1, :], s_col[:, :], wsc[:, 3, w:w + 1], None, ALU.mult)
                ins.then_inc(norm_step, 1)
                dve.wait_ge(norm_step, NORM_STEPS * (g + 1))

            def u_low(n, rs):
                for r in rs:
                    q = RT * n + r
                    dve.wait_ge(split_hi, VP + q + 1)
                    stt(u_hl[:, n, r, 1, :], u_bank(q)[:, :], us_scale[:, n, r:r + 1], u_hl[:, n, r, 0, :],
                        ALU.mult, ALU.subtract).then_inc(split_lo, 1)

            def stage2_block(u):
                q, t = u + 2 < NT, u + 2
                cs = boundary_chunks(u)
                if u % TB == 0:
                    for p in range(3):
                        norm_piece(u, p)
                if not has_s1(u):
                    norm_piece(u, 3)
                for p in range(NQ):
                    if has_s1(u) and p < 3:
                        x1_unit(u + 1, p)
                    lo(u, p)
                    if p == 0 and has_s1(u):
                        norm_piece(u, 3)
                    if p > 0:
                        chunks(cs[p - 1])
                if u % TB == 0 and u > 0:
                    x1_unit(u + 1, NQ - 2)
                if u == 0:
                    u_norm(1)
                    for n in range(NQ):
                        u_low(n, (0, 1))
                        if n == 2:
                            u_norm(2)
                        u_low(n, (2, 3))
                        if n == 0:
                            stats1(2)
                        if n == 1:
                            x1_unit(1, NQ - 2)
                if q and u > 0:
                    stats1(t)
                chunks(cs[3])
                lo(u, NQ)
                chunks(cs[4])
                if q:
                    for j in range(3):
                        round_piece(t, j)
                if has_last(u):
                    x1_unit(u + 1, NQ - 1)
                for n in range(NQ):
                    if n == NQ - 1 and (u + 1) % TB:
                        for p in range(3):
                            norm_piece(u + 1, p)
                    y_unit(u, n)
                    if q and n < 2:
                        qT_piece(t, n)
                    if q and n == 2:
                        qT_piece(t, 2)
                        qT_piece(t, 3)
                        row_correction(t)
                    chunks(cs[5 + n])
                    if q and n == 0:
                        round_piece(t, 3)
                    if has_last(u) and n == 0:
                        stats2(u + 1)

            stats1_sums(0)
            first_constants()
            for b in range(NB):
                pair(b)
                for u in range(TB * b, TB * b + TB):
                    stage2_block(u)


_INS = ['x', 'ctx_4096', 'g_xattn', 'g_ffn', 'L0_xattn_x1_scale', 'L0_xattn_x1_zp', 'L0_xattn_x2_scale',
        'L0_xattn_x2_zp', 'L0_ffn_U', 'L0_ffn_S', 'L0_ffn_V']
_OUTS = [((2, 1024, 2048), 'float32')]


def kernel(**inputs):
    import numpy as _np
    import concourse.bacc as _bacc
    from concourse import mybir as _mybir
    from concourse.bass_utils import run_bass_kernel_spmd as _run

    nc = _bacc.Bacc("TRN2", target_bir_lowering=False, num_devices=1)
    arrays, args = {}, []
    for name in _INS:
        a = _np.ascontiguousarray(inputs[name])
        arrays[f"in_{name}_dram"] = a
        args.append(nc.dram_tensor(f"in_{name}_dram", a.shape, _mybir.dt.from_np(a.dtype), kind="ExternalInput").ap())
    for i, (shape, dtype) in enumerate(_OUTS):
        dt = _mybir.dt.from_np(_np.dtype(dtype))
        args.append(nc.dram_tensor(f"out_{i}_dram", shape, dt, kind="ExternalOutput").ap())
    gated_block_program(nc, *args)
    r = _run(nc, [arrays], core_ids=[0])
    return r.results[0]["out_0_dram"]
```
